# Optimizing a Trainium2 kernel written in Bass

```python
import numpy as np
import jax
import jax.numpy as jnp

def _softmax(x, axis=-1):
    return jax.nn.softmax(x, axis=axis)

def _gelu(x):
    return jax.nn.gelu(x, approximate=True)

def _silu(x):
    return jax.nn.silu(x)

def _sigmoid(x):
    return jax.nn.sigmoid(x)

def _layernorm(x, axis=-1, eps=1e-05):
    m = jnp.mean(x, axis=axis, keepdims=True)
    v = jnp.var(x, axis=axis, keepdims=True)
    return (x - m) / jnp.sqrt(v + eps)

def _scatter_add(tgt, idx, src, axis=0):
    return tgt.at[idx].add(src)

def _segment_sum(src, seg, n):
    return jax.ops.segment_sum(src, seg, n)
kernel_name = 'mk_prb_d1_jaxref_r8_76b629'

def setup_inputs(seed: int=0):
    np.random.seed(seed)
    _w = jnp.asarray

    def _L0_attn_setup():
        import math
        import jax, jax.numpy as jnp
        import numpy as np
        NUM_BUCKETS = 32
        MAX_DISTANCE = 128
        HEADS = 16
        D_MODEL = 128
        SEQ = 128
        BATCH = 4
        SCALE = (D_MODEL // HEADS) ** (-0.5)

        def _rel_pos_bucket_causal(seq_len):
            pos = jnp.arange(seq_len)
            n = jnp.maximum(pos[:, None] - pos[None, :], 0)
            max_exact = NUM_BUCKETS // 2
            val_large = max_exact + (jnp.log(jnp.maximum(n, 1).astype(jnp.float32) / max_exact) / math.log(MAX_DISTANCE / max_exact) * (NUM_BUCKETS - max_exact)).astype(jnp.int32)
            val_large = jnp.minimum(val_large, NUM_BUCKETS - 1)
            return jnp.where(n < max_exact, n, val_large)
        key = jax.random.key(seed)
        ks = jax.random.split(key, 6)
        s = 0.02
        return {'x': jax.random.normal(ks[0], (BATCH, SEQ, D_MODEL), jnp.float32), 'Wq': jax.random.normal(ks[1], (D_MODEL, D_MODEL), jnp.float32) * s, 'bq': jnp.zeros((D_MODEL,), jnp.float32), 'Wk': jax.random.normal(ks[2], (D_MODEL, D_MODEL), jnp.float32) * s, 'bk': jnp.zeros((D_MODEL,), jnp.float32), 'Wv': jax.random.normal(ks[3], (D_MODEL, D_MODEL), jnp.float32) * s, 'bv': jnp.zeros((D_MODEL,), jnp.float32), 'Wo': jax.random.normal(ks[4], (D_MODEL, D_MODEL), jnp.float32) * s, 'bo': jnp.zeros((D_MODEL,), jnp.float32), 'rel_emb': jax.random.normal(ks[5], (NUM_BUCKETS, HEADS), jnp.float32) * s}
    _L0_attn_in = _L0_attn_setup()

    def _L0_ffn_setup():
        import jax, jax.numpy as jnp
        import numpy as np
        SWIGLU_ALPHA = 1.702
        SWIGLU_LIMIT = 7.0
        TOP_K = 4
        key = jax.random.key(seed)
        k = jax.random.split(key, 5)
        B, S, D, E, I = (2, 128, 128, 8, 256)
        return {'hidden_states': jax.random.normal(k[0], (B, S, D), dtype=jnp.float32), 'router_weight': jax.random.normal(k[1], (E, D), dtype=jnp.float32) * 0.02, 'router_bias': jnp.zeros((E,), dtype=jnp.float32), 'gate_up_proj': jax.random.normal(k[2], (E, 2 * I, D), dtype=jnp.float32) * 0.02, 'gate_up_proj_bias': jnp.zeros((E, 2 * I), dtype=jnp.float32), 'down_proj': jax.random.normal(k[3], (E, D, I), dtype=jnp.float32) * 0.02, 'down_proj_bias': jnp.zeros((E, D), dtype=jnp.float32)}
    _L0_ffn_in = _L0_ffn_setup()
    _d = {'L0_attn_x': _L0_attn_in['x'], 'L0_attn_Wq': _L0_attn_in['Wq'], 'L0_attn_bq': _L0_attn_in['bq'], 'L0_attn_Wk': _L0_attn_in['Wk'], 'L0_attn_bk': _L0_attn_in['bk'], 'L0_attn_Wv': _L0_attn_in['Wv'], 'L0_attn_bv': _L0_attn_in['bv'], 'L0_attn_Wo': _L0_attn_in['Wo'], 'L0_attn_bo': _L0_attn_in['bo'], 'L0_attn_rel_emb': _L0_attn_in['rel_emb'], 'L0_ffn_router_weight': _L0_ffn_in['router_weight'], 'L0_ffn_router_bias': _L0_ffn_in['router_bias'], 'L0_ffn_gate_up_proj': _L0_ffn_in['gate_up_proj'], 'L0_ffn_gate_up_proj_bias': _L0_ffn_in['gate_up_proj_bias'], 'L0_ffn_down_proj': _L0_ffn_in['down_proj'], 'L0_ffn_down_proj_bias': _L0_ffn_in['down_proj_bias']}
    _x0 = _d['L0_attn_x']
    _d['L0_attn_x'] = jax.random.normal(jax.random.fold_in(jax.random.key(seed), 1), (16, 256, 128), dtype=_x0.dtype)
    del _x0
    return _d

def reference(L0_attn_x, L0_attn_Wq, L0_attn_bq, L0_attn_Wk, L0_attn_bk, L0_attn_Wv, L0_attn_bv, L0_attn_Wo, L0_attn_bo, L0_attn_rel_emb, L0_ffn_router_weight, L0_ffn_router_bias, L0_ffn_gate_up_proj, L0_ffn_gate_up_proj_bias, L0_ffn_down_proj, L0_ffn_down_proj_bias):

    def _L0_attn_ref(x, Wq, bq, Wk, bk, Wv, bv, Wo, bo, rel_emb):
        import math
        import jax, jax.numpy as jnp
        import numpy as np
        NUM_BUCKETS = 32
        MAX_DISTANCE = 128
        HEADS = 16
        D_MODEL = 128
        SEQ = 128
        BATCH = 4
        SCALE = (D_MODEL // HEADS) ** (-0.5)

        def _rel_pos_bucket_causal(seq_len):
            pos = jnp.arange(seq_len)
            n = jnp.maximum(pos[:, None] - pos[None, :], 0)
            max_exact = NUM_BUCKETS // 2
            val_large = max_exact + (jnp.log(jnp.maximum(n, 1).astype(jnp.float32) / max_exact) / math.log(MAX_DISTANCE / max_exact) * (NUM_BUCKETS - max_exact)).astype(jnp.int32)
            val_large = jnp.minimum(val_large, NUM_BUCKETS - 1)
            return jnp.where(n < max_exact, n, val_large)
        b, n, d = x.shape
        h, hd = (HEADS, d // HEADS)
        q = (x @ Wq.T + bq).reshape(b, n, h, hd).transpose(0, 2, 1, 3)
        k = (x @ Wk.T + bk).reshape(b, n, h, hd).transpose(0, 2, 1, 3)
        v = (x @ Wv.T + bv).reshape(b, n, h, hd).transpose(0, 2, 1, 3)
        sim = jnp.einsum('bhid,bhjd->bhij', q, k)
        rp_bucket = _rel_pos_bucket_causal(n)
        bias = rel_emb[rp_bucket]
        sim = sim + jnp.transpose(bias, (2, 0, 1)) * SCALE
        i = jnp.arange(n)
        causal = jnp.where(i[None, :] > i[:, None], -jnp.inf, 0.0).astype(sim.dtype)
        sim = sim + causal
        attn = jax.nn.softmax(sim, axis=-1)
        out = jnp.einsum('bhij,bhjd->bhid', attn, v)
        out = out.transpose(0, 2, 1, 3).reshape(b, n, d)
        return out @ Wo.T + bo

    def _L0_ffn_ref(hidden_states, router_weight, router_bias, gate_up_proj, gate_up_proj_bias, down_proj, down_proj_bias):
        import jax, jax.numpy as jnp
        import numpy as np
        SWIGLU_ALPHA = 1.702
        SWIGLU_LIMIT = 7.0
        TOP_K = 4
        B, S, D = hidden_states.shape
        E = router_weight.shape[0]
        x = hidden_states.reshape(-1, D)
        N = x.shape[0]
        logits = x @ router_weight.T + router_bias
        topk_logits, topk_idx = jax.lax.top_k(logits, TOP_K)
        topk_w = jax.nn.softmax(topk_logits.astype(jnp.float32), axis=-1)
        combine = jnp.zeros((N, E), dtype=jnp.float32)
        combine = combine.at[jnp.arange(N)[:, None], topk_idx].set(topk_w)
        gate_up = jnp.einsum('nd,ejd->nej', x, gate_up_proj) + gate_up_proj_bias
        gate, up = jnp.split(gate_up, 2, axis=-1)
        gate = jnp.minimum(gate, SWIGLU_LIMIT)
        up = jnp.clip(up, -SWIGLU_LIMIT, SWIGLU_LIMIT)
        act = (up + 1.0) * gate * jax.nn.sigmoid(SWIGLU_ALPHA * gate)
        out = jnp.einsum('nei,edi->ned', act, down_proj) + down_proj_bias
        y = jnp.einsum('ned,ne->nd', out, combine.astype(out.dtype))
        return y.reshape(B, S, D)
    x = L0_attn_x
    xn = _layernorm(x, axis=-1)
    x = x + _L0_attn_ref(xn, L0_attn_Wq, L0_attn_bq, L0_attn_Wk, L0_attn_bk, L0_attn_Wv, L0_attn_bv, L0_attn_Wo, L0_attn_bo, L0_attn_rel_emb) + _L0_ffn_ref(xn, L0_ffn_router_weight, L0_ffn_router_bias, L0_ffn_gate_up_proj, L0_ffn_gate_up_proj_bias, L0_ffn_down_proj, L0_ffn_down_proj_bias)
    return x

_drawn_inputs = setup_inputs


def setup_inputs(seed=0):
    import zlib

    import numpy as np

    out = dict(_drawn_inputs(seed))
    spreads = {'L0_attn_bq': (0.0, 0.8),
     'L0_attn_bk': (0.0, 2.0),
     'L0_attn_bv': (0.0, 0.382),
     'L0_attn_bo': (0.0, 0.1),
     'L0_ffn_router_bias': (0.0, 0.329),
     'L0_ffn_gate_up_proj_bias': (0.0, 0.8),
     'L0_ffn_down_proj_bias': (0.0, 0.1)}
    factors = {'L0_attn_Wq': 8.0,
     'L0_attn_Wk': 8.0,
     'L0_attn_Wv': 7.079,
     'L0_attn_rel_emb': 64.0,
     'L0_ffn_gate_up_proj': 2.869}
    for name, (base, spread) in spreads.items():
        noise = np.random.default_rng([zlib.crc32(name.encode()), seed]).standard_normal(out[name].shape)
        drawn = base * np.exp(spread * noise) if base else spread * noise
        out[name] = jnp.asarray(drawn.astype(out[name].dtype))
    for name, factor in factors.items():
        out[name] = (out[name] * factor).astype(out[name].dtype)
    return out
```

```python
from contextlib import ExitStack
import math

import numpy as np

import concourse.bass as bass
from concourse import mybir

F32 = mybir.dt.float32
F32R = mybir.dt.float32r
ACT = mybir.ActivationFunctionType
ALU = mybir.AluOpType
AX = mybir.AxisListType

P = 128
HEADS, HD = 16, 8
NG = 4
BUCKETS, MAX_DISTANCE = 32, 128
SCALE = HD ** -0.5
EPS = 1e-5
EXPERTS, TOP_K, INTER = 8, 4, 256
ALPHA, LIMIT = 1.702, 7.0
CLIP = ALPHA * LIMIT / (1.0 + math.exp(-ALPHA * LIMIT))
MASKED = -1.0e30
SPAN = 384
SEQ = 256
T = 512
TILES = T // P
CHUNKS = EXPERTS * INTER // P
LAG = 4
SU_SLOTS, AW_SLOTS, P_SLOTS = 3, 4, 8


class Count:

    def __init__(self, per, by=1):
        self.per, self.by, self.base, self.local, self.t = per, by, 0, 0, None

    def begin(self, t):
        if self.t is None:
            self.base = self.local
        else:
            assert self.local in (0, self.per), (self.local, self.per)
        self.t, self.local = t, 0

    def step(self, n=1):
        self.local += n
        return self.now()

    def now(self):
        if self.t is None:
            return self.local * self.by
        return self.t * (self.per * self.by) + (self.base + self.local) * self.by


def build_layer(nc, ins, out, steps):
    ctx = ExitStack()
    with ctx:
        def sb(name, shape, dt=F32):
            return ctx.enter_context(nc.sbuf_tensor(name, shape, dt))

        def bank(name):
            return ctx.enter_context(nc.psum_tensor(name, [P, 512], F32))

        def sem(name):
            return ctx.enter_context(nc.semaphore(name))

        ident = sb("ident", [P, P])
        ident_r = sb("ident_r", [P, P], F32R)
        wqk_hi = sb("wqk_hi", [P, 2, P], F32R)
        wqk_lo = sb("wqk_lo", [P, 2, P], F32R)
        wv = sb("wv", [P, P])
        wo_t = sb("wo_t", [P, P])
        wr_t = sb("wr_t", [P, EXPERTS])
        gu_hi = sb("gu_hi", [P, 4096], F32R)
        gu_lo = sb("gu_lo", [P, 4096], F32R)
        dn_t = sb("dn_t", [P, CHUNKS, P])
        dn_bias = sb("dn_bias", [EXPERTS, P])
        gu_bias = sb("gu_bias", [P, 32])
        gate_bias = sb("gate_bias", [P, 32])
        up_bias = sb("up_bias", [P, 32])
        cols = sb("cols", [P, 3])
        bv_rows = sb("bv_rows", [P, P])
        rb_rows = sb("rb_rows", [P, EXPERTS])
        tri = sb("tri", [P, TILES * 64])
        rel = sb("rel", [BUCKETS, HEADS])
        bias_hi = sb("bias_hi", [P, HEADS, 384], F32R)
        bias_lo = sb("bias_lo", [P, HEADS, 384], F32R)
        minus_half = sb("minus_half", [P, TILES])
        x_in = sb("x_in", [P, TILES, P])
        x_res = sb("x_res", [P, TILES, P])
        stats = sb("stats", [P, TILES, 6])
        mean_var = sb("mean_var", [P, TILES, 2])
        var_eps = sb("var_eps", [P, TILES])
        rstd = sb("rstd", [P, TILES])
        xn = sb("xn", [P, TILES, P])
        attn_t = xn[:, :, :].rearrange("p q c -> p (q c)")
        xn_t = sb("xn_t", [P, T])
        y_t = xn_t
        xn_rev = sb("xn_rev", [P, T])
        xn_hi = sb("xn_hi", [P, T], F32R)
        xn_lo = sb("xn_lo", [P, T], F32R)
        qk_hi = sb("qk_hi", [P, 2, T], F32R)
        qk_lo = sb("qk_lo", [P, 2, T], F32R)
        q_rows = sb("q_rows", [P, NG, T], F32R)
        k_rows = sb("k_rows", [P, NG, T], F32R)
        v_one = sb("v_one", [P, TILES, HEADS * (HD + 1) + 32])
        v_heads = v_one[:, :, 0:HEADS * (HD + 1)].rearrange("p q (h w) -> p q h w", h=HEADS)
        row_max = sb("row_max", [P, TILES, HEADS])
        neg_max = sb("neg_max", [HEADS, T])
        soft = sb("soft", [P, P_SLOTS * 384 + NG * T])
        probs = soft[:, 0:P_SLOTS * 384].rearrange("p (s c) -> p s c", s=P_SLOTS)
        heads_t = soft[:, P_SLOTS * 384:].rearrange("p (g t) -> p g t", g=NG)
        bias_raw = soft[:, 0:4096].rearrange("p (h c) -> p h c", h=HEADS)
        recip = sb("recip", [P, TILES, HEADS])
        attn = x_in
        logits = sb("logits", [P, TILES, EXPERTS])
        shifted = sb("shifted", [P, TILES, EXPERTS])
        exps = sb("exps", [P, TILES * EXPERTS])
        top = sb("top", [P, TILES])
        diff = sb("diff", [P, TILES * 64])
        ahead = sb("ahead", [P, TILES * 64])
        rank = sb("rank", [P, TILES * EXPERTS])
        kept = sb("kept", [P, TILES * EXPERTS])
        total = sb("total", [P, TILES])
        total_inv = sb("total_inv", [P, TILES])
        combine = sb("combine", [P, TILES, EXPERTS])
        comb_t = sb("comb_t", [EXPERTS, T])
        comb_scaled = neg_max[0:EXPERTS, :]
        comb_all = sb("comb_all", [P, EXPERTS, T])
        gu_raw = comb_all[:, :, :].rearrange("p e t -> p (e t)")
        s_buf = sb("s_buf", [P, SU_SLOTS, T])
        u_buf = sb("u_buf", [P, SU_SLOTS, T])
        aw_buf = sb("aw_buf", [P, AW_SLOTS, T])
        wqk = aw_buf[:, 0, 0:2 * P].rearrange("p (w c) -> p w c", w=2)
        onehot = aw_buf[0:BUCKETS, 1, 0:SPAN]
        dist = aw_buf[0:HEADS, 3, 0:SPAN]
        dist_dram = nc.dram_tensor("dist_dram", [HEADS, SPAN], F32, kind="Internal")

        class Bank:

            def __init__(self, name, per):
                self.ps, self.full, self.free, self.per = bank(name), sem(name + "_full"), sem(name + "_free"), per

        GATE = Bank("gate", 1 + CHUNKS)
        UP = Bank("up", 1 + CHUNKS)
        S = [Bank("scores0", 32), Bank("scores1", 32)]
        PV = Bank("pv", 8)
        Y = Bank("y", 1)
        M0 = Bank("misc0", 7)
        M1 = Bank("misc1", 6)
        BANKS = [GATE, UP, *S, PV, Y, M0, M1]

        w_loaded = {n: sem(n + "_loaded") for n in ("attn_w", "small", "gu", "dn", "hot", "bias_raw", "x", "x_res")}
        dist_ready, dist_stored = sem("dist_ready"), sem("dist_stored")
        filled = sem("filled")
        attn_w_hi, attn_w_split = sem("attn_w_hi"), sem("attn_w_split")
        gu_hi_done, gu_split = sem("gu_hi_done"), sem("gu_split")
        bias_hi_done, bias_split = sem("bias_hi_done"), sem("bias_split")
        biases_ready, ident_ready = sem("biases_ready"), sem("ident_ready")
        var_ready, rstd_ready, xn_ready = sem("var_ready"), sem("rstd_ready"), sem("xn_ready")
        xn_split = sem("xn_split")
        qk_hi_done = sem("qk_hi_done")
        rows_loaded, max_loaded = sem("rows_loaded"), [sem("max0_loaded"), sem("max1_loaded")]
        shifted_ready, exps_ready, combine_ready = sem("shifted_ready"), sem("exps_ready"), sem("combine_ready")
        comb_row_loaded, comb_all_ready = sem("comb_row_loaded"), sem("comb_all_ready")
        act_ready, weighted, down_done = sem("act_ready"), sem("weighted"), sem("down_done")
        stored = sem("stored")
        dve_step, pool_step = sem("dve_step"), sem("pool_step")
        DVE_STEPS = 0 if steps is None else steps["dve"]
        x_view = ins["x"].rearrange("(n q p) c -> n p q c", p=P, q=TILES)
        out_view = out.rearrange("(n q p) c -> n p q c", p=P, q=TILES)
        N = x_view.shape[0]

        def units(first, last):
            return [(u, u // 16, u % 4, u % 16 // 4) for u in range(first, last)]

        class Program:

            def __init__(self, eng):
                self.eng = eng
                self.uses = {id(b): Count(b.per) for b in BANKS}
                self.counts = {}
                self.value = None

            def count(self, s, per, by=1):
                return self.counts.setdefault(id(s), Count(per, by))

            def begin(self, t):
                for c in [*self.uses.values(), *self.counts.values()]:
                    c.begin(t)

            def wait(self, s, n):
                if not isinstance(n, int):
                    self.value = self.value or self.eng.alloc_register("awaited")
                    self.eng.reg_add(self.value, n, 0)
                    self.eng.wait_ge(dist_ready, 1)
                    n = self.value
                self.eng.wait_ge(s, n)

            def fill(self, b):
                n = self.uses[id(b)].step() - 1
                if not isinstance(n, int) or n > 0:
                    self.eng.wait_ge(b.free, n)

            def read(self, b, apart=False):
                n = self.uses[id(b)].step()
                (self.wait if apart else self.eng.wait_ge)(b.full, n)

            def skip(self, b, n=1):
                return self.uses[id(b)].step(n)

        block = ctx.enter_context(nc.Block())

        @block.sync
        def _(sp):
            pr = Program(sp)
            xn_ready_n = pr.count(xn_ready, 1)
            stored_n = pr.count(stored, 1, 16)
            weighted_n = pr.count(weighted, CHUNKS)
            small = [(ident[:], ins["ident"]), (cols[:], ins["cols"]), (wr_t[:], ins["wr_t"]),
                     (rb_rows[:], ins["rb"].partition_broadcast(P)), (bv_rows[:], ins["bv"].partition_broadcast(P)),
                     (tri[:], ins["tri"].partition_broadcast(P)), (dn_bias[:], ins["dn_bias"]),
                     (gu_bias[:], ins["gu_bias"]), (wo_t[:], ins["wo_t"]), (wv[:], ins["wv"])]
            sp.dma_start(x_in[:], x_view[0]).then_inc(w_loaded["x"], 16)
            sp.dma_start(rel[:], ins["rel"]).then_inc(w_loaded["hot"], 16)
            sp.dma_start(onehot, ins["onehot"]).then_inc(w_loaded["hot"], 16)
            sp.dma_start(wqk, ins["wqk"]).then_inc(w_loaded["attn_w"], 16)
            for dst, src in small:
                sp.dma_start(dst, src).then_inc(w_loaded["small"], 16)
            for c in range(8):
                sp.dma_start(gu_raw[:, 512 * c:512 * c + 512], ins["gu_t"][:, 512 * c:512 * c + 512]).then_inc(w_loaded["gu"], 16)
            sp.wait_ge(dist_ready, 1)
            sp.dma_start(dist_dram.ap(), dist).then_inc(dist_stored, 16)
            sp.wait_ge(dist_stored, 16)
            sp.dma_start(bias_raw, bass.AP(dist_dram, 0, [[1, P], [SPAN, HEADS], [1, 256]])).then_inc(w_loaded["bias_raw"], 16)
            sp.dma_start(dn_t[:], ins["dn_t"]).then_inc(w_loaded["dn"], 16)
            sp.dma_start(x_res[:], x_view[0]).then_inc(w_loaded["x_res"], 16)

            def load_comb_row():
                pr.wait(M1.free, pr.skip(M1))
                if pr.uses[id(M1)].t is not None:
                    pr.wait(weighted, weighted_n.now())
                else:
                    sp.wait_ge(gu_split, 8)
                sp.dma_start(comb_all[0:1, :, :], comb_scaled).then_inc(comb_row_loaded, 16)

            def load_rows():
                pr.wait(GATE.free, pr.skip(GATE))
                pr.wait(UP.free, pr.skip(UP))
                for rows, which, parts in ((q_rows, 0, (qk_hi, qk_hi, qk_lo)), (k_rows, 1, (qk_hi, qk_lo, qk_hi))):
                    for a, part in enumerate(parts):
                        sp.dma_start(rows[a:P:4].bitcast(F32), part[:, which, :].bitcast(F32)).then_inc(rows_loaded, 16)

            pr.skip(M1, 0)
            load_comb_row()
            sp.wait_ge(filled, 4)
            load_rows()
            pr.skip(M1)

            def body(t, last):
                pr.begin(t)
                if not last:
                    pr.wait(xn_ready, xn_ready_n.step())
                    sp.dma_start(x_in[:], x_view[t + 1]).then_inc(w_loaded["x"], 16)
                pr.skip(GATE, CHUNKS - LAG)
                pr.skip(UP, CHUNKS - LAG)
                for b in range(2):
                    pr.wait(M1.free, pr.skip(M1))
                    sp.dma_start(q_rows[31:P:32, :, b * SEQ:b * SEQ + SEQ].bitcast(F32),
                                 neg_max[:, b * SEQ:b * SEQ + SEQ]).then_inc(max_loaded[b], 16)
                weighted_n.step(CHUNKS - LAG)
                if not last:
                    load_comb_row()
                    weighted_n.step(LAG)
                    for b in range(2):
                        pr.wait(S[b].full, pr.skip(S[b], 32))
                    load_rows()
                    pr.skip(M1)
                    pr.skip(GATE, LAG)
                    pr.skip(UP, LAG)
                pr.skip(M1, 2)
                pr.wait(M0.free, pr.skip(M0, 7 if not last else 5))
                sp.dma_start(out_view[t], x_res[:]).then_inc(stored, 16)
                stored_n.step()
                pr.wait(stored, stored_n.now())
                if not last:
                    sp.dma_start(x_res[:], x_view[t + 1]).then_inc(w_loaded["x_res"], 16)

            pr.skip(M0, 2)
            pr.skip(GATE, LAG)
            pr.skip(UP, LAG)
            weighted_n.step(LAG)
            pr.skip(S[0])
            with sp.Fori(0, N - 1) as t:
                body(t, False)
            body(N - 1, True)

        @block.tensor
        def _(pe):
            pr = Program(pe)
            xn_ready_n, xn_split_n = pr.count(xn_ready, 1), pr.count(xn_split, 1)
            rows_n, max_n = pr.count(rows_loaded, 6, 16), [pr.count(m, 1, 16) for m in max_loaded]
            comb_n, weighted_n = pr.count(combine_ready, 1), pr.count(weighted, CHUNKS)
            freed = {}

            def split_product(dst, hi, lo, rhs_hi, rhs_lo):
                nc.tensor.matmul(dst, lo, rhs_hi, start=True, stop=False)
                nc.tensor.matmul(dst, hi, rhs_lo, start=False, stop=False)
                return nc.tensor.matmul(dst, hi, rhs_hi, start=False, stop=True)

            def transpose_x():
                pr.fill(M0)
                pe.wait_ge(xn_ready, xn_ready_n.step())
                for q in range(TILES):
                    mm = nc.tensor.transpose(M0.ps[:, q * P:q * P + P], xn[:, q, :], ident[:])
                mm.then_inc(M0.full, 1)
                freed["xn_t"] = pr.uses[id(M0)].now()

            def router():
                pe.wait_ge(M0.free, freed["xn_t"])
                pr.fill(M0)
                for q in range(TILES):
                    mm = nc.tensor.matmul(M0.ps[:, q * EXPERTS:(q + 1) * EXPERTS], xn_t[:, q * P:q * P + P], wr_t[:],
                                          start=True, stop=True)
                mm.then_inc(M0.full, 1)

            def project_qk():
                pe.wait_ge(xn_split, xn_split_n.step())
                pr.fill(GATE)
                split_product(GATE.ps[:], wqk_hi[:, 0, :], wqk_lo[:, 0, :], xn_hi[:], xn_lo[:]).then_inc(GATE.full, 1)
                pr.fill(UP)
                split_product(UP.ps[:], wqk_hi[:, 1, :], wqk_lo[:, 1, :], xn_hi[:, ::-1], xn_lo[:, ::-1]).then_inc(UP.full, 1)

            def project_v():
                pr.fill(M1)
                for q in range(TILES):
                    mm = nc.tensor.matmul(M1.ps[:, q * P:q * P + P], xn_rev[:, q * P:q * P + P], wv[:], start=True, stop=True)
                mm.then_inc(M1.full, 1)

            def transpose_combine():
                pr.fill(M1)
                pe.wait_ge(combine_ready, comb_n.step())
                for q in range(TILES):
                    mm = nc.tensor.transpose(M1.ps[0:EXPERTS, q * P:q * P + P], combine[:, q, :], ident[:])
                mm.then_inc(M1.full, 1)
                freed["comb_t"] = pr.uses[id(M1)].local, pr.uses[id(M1)].now()

            def gate_up(k):
                e, c = divmod(k, 2)
                for b, half in ((GATE, 0), (UP, 1)):
                    w = slice(e * 512 + half * 256 + c * P, e * 512 + half * 256 + c * P + P)
                    pr.fill(b)
                    split_product(b.ps[:], gu_hi[:, w], gu_lo[:, w], xn_hi[:], xn_lo[:]).then_inc(b.full, 1)

            def down(k):
                if k == 0:
                    pr.fill(Y)
                    nc.tensor.matmul(Y.ps[:], dn_bias[:], comb_t[:], start=True, stop=False)
                pe.wait_ge(weighted, weighted_n.step())
                nc.tensor.matmul(Y.ps[:], dn_t[:, k, :], aw_buf[:, k % AW_SLOTS, :], start=False, stop=False).then_inc(down_done, 1)

            def max_scores(u, b, r, g):
                s = S[u % 2]
                pr.fill(s)
                rows = slice(32 * r, 32 * r + 31)
                q, k = q_rows[rows, g, b * SEQ:(b + 1) * SEQ], k_rows[rows, g, (1 - b) * SEQ:(2 - b) * SEQ]
                nc.tensor.matmul(s.ps[:, 0:P], q[:, 0:P], k[:, P:SEQ], start=True, stop=True)
                mm = nc.tensor.matmul(s.ps[:, P:P + SEQ], q[:, P:SEQ], k, start=True, stop=True)
                mm.then_inc(s.full, 1)

            def transpose_max(b):
                for s in S:
                    pe.wait_ge(s.free, pr.uses[id(s)].now())
                pr.fill(M1)
                for q in range(2):
                    mm = nc.tensor.transpose(M1.ps[0:HEADS, q * P:q * P + P], row_max[:, 2 * b + q, :], ident[:])
                mm.then_inc(M1.full, 1)

            def prob_scores(u, b, r, g):
                s = S[u % 2]
                pr.fill(s)
                rows = slice(32 * r, 32 * r + 32)
                h = 4 * r + g
                nc.tensor.matmul(s.ps[:, 0:384], ident_r[:], bias_lo[:, h, :], start=True, stop=False)
                nc.tensor.matmul(s.ps[:, 0:384], ident_r[:], bias_hi[:, h, :], start=False, stop=False)
                q, k = q_rows[rows, g, b * SEQ:(b + 1) * SEQ], k_rows[rows, g, (1 - b) * SEQ:(2 - b) * SEQ]
                nc.tensor.matmul(s.ps[:, 0:SEQ], k[:, P:SEQ], q, start=False, stop=False)
                nc.tensor.matmul(s.ps[:, SEQ:SEQ + P], k[:, 0:P], q[:, P:SEQ], start=False, stop=True).then_inc(s.full, 1)

            def weigh_values(grp, now):
                b, g = divmod(grp, 4)
                for s, v in zip(S, now):
                    pe.wait_ge(s.free, v)
                pr.fill(PV)
                for kt in range(2):
                    for r in range(4):
                        p = probs[:, (4 * grp + r) % P_SLOTS, :]
                        dst = PV.ps[32 * r:32 * r + 32, kt * P:256]
                        mm = nc.tensor.matmul(dst, v_one[:, 2 * (1 - b) + 1 - kt, (4 * r + g) * (HD + 1):(4 * r + g) * (HD + 1) + 32], p[:, 256 * kt:256 + 128 * kt],
                                              start=(kt == 0), stop=(kt == 1), tile_position=(0, 32 * r))
                mm.then_inc(PV.full, 1)

            def transpose_heads(q):
                pr.fill(M0)
                pe.wait_ge(PV.free, freed["heads", q // 2])
                for g in range(NG):
                    mm = nc.tensor.transpose(M0.ps[:, g * P:g * P + P], heads_t[:, g, q * P:q * P + P], ident[:])
                mm.then_inc(M0.full, 1)
                freed[("norm", q)] = pr.uses[id(M0)].now()

            def transpose_attn(b):
                pe.wait_ge(M0.free, freed[("norm", 2 * b + 1)])
                pr.fill(M1)
                for q in range(2):
                    mm = nc.tensor.transpose(M1.ps[:, q * P:q * P + P], attn[:, 2 * b + q, :], ident[:])
                mm.then_inc(M1.full, 1)
                freed[("attn_t", b)] = pr.uses[id(M1)].now()

            def project_out():
                pe.wait_ge(M1.free, freed[("attn_t", 1)])
                nc.tensor.matmul(Y.ps[:], wo_t[:], attn_t, start=False, stop=True).then_inc(Y.full, 1)

            def transpose_y():
                pr.fill(M0)
                pe.wait_ge(Y.free, pr.uses[id(Y)].now())
                for q in range(TILES):
                    mm = nc.tensor.transpose(M0.ps[:, q * P:q * P + P], y_t[:, q * P:q * P + P], ident[:])
                mm.then_inc(M0.full, 1)

            pe.wait_ge(w_loaded["hot"], 32)
            pr.fill(S[0])
            nc.tensor.matmul(S[0].ps[0:HEADS, 0:SPAN], rel[:], onehot, start=True, stop=True).then_inc(S[0].full, 1)
            pe.wait_ge(w_loaded["small"], 16 * 10)
            transpose_x()
            pe.wait_ge(attn_w_split, 1)
            router()
            project_qk()
            transpose_combine()
            project_v()
            pe.wait_ge(ident_ready, 1)
            for k in range(LAG):
                if k % 2 == 0:
                    pe.wait_ge(gu_split, k // 2 + 1)
                gate_up(k)

            def body(t, last):
                pr.begin(t)
                todo = units(0, 32)
                pe.wait_ge(rows_loaded, rows_n.step(6))
                for k in range(LAG, CHUNKS):
                    if k % 2 == 0:
                        pe.wait_ge(gu_split, k // 2 + 1)
                    if k == LAG:
                        pe.wait_ge(w_loaded["dn"], 16)
                    gate_up(k)
                    for u in todo[:3]:
                        max_scores(*u)
                    if k == 10:
                        transpose_max(0)
                    todo = todo[3:]
                    down(k - LAG)
                assert not todo
                transpose_max(1)
                pe.wait_ge(bias_split, 1)
                free_at, pv_at = [], []
                for grp in range(8):
                    if grp % 4 == 0:
                        pe.wait_ge(max_loaded[grp // 4], max_n[grp // 4].step())
                    if grp < LAG:
                        down(CHUNKS - LAG + grp)
                    for u in units(4 * grp, 4 * grp + 4):
                        prob_scores(*u)
                    free_at.append([pr.uses[id(s)].now() for s in S])
                    if grp:
                        weigh_values(grp - 1, free_at[grp - 1])
                        pv_at.append(pr.uses[id(PV)].now())
                    if grp == 1 and not last:
                        transpose_x()
                    if grp == 3 and not last:
                        router()
                        project_qk()
                    if grp == 5:
                        freed["heads", 0] = pv_at[3]
                        transpose_heads(0)
                    if grp == 6:
                        transpose_heads(1)
                        if not last:
                            transpose_combine()
                    if grp == 7:
                        transpose_attn(0)
                weigh_values(7, free_at[7])
                freed["heads", 1] = pr.uses[id(PV)].now()
                if not last:
                    project_v()
                    gate_up(0)
                transpose_heads(2)
                transpose_heads(3)
                if not last:
                    gate_up(1)
                transpose_attn(1)
                if not last:
                    gate_up(2)
                project_out()
                if not last:
                    gate_up(3)
                transpose_y()

            with pe.Fori(0, N - 1) as t:
                body(t, False)
            body(N - 1, True)

        @block.scalar
        def _(act):
            pr = Program(act)
            shifted_n = pr.count(shifted_ready, 1)
            act_n, weighted_n = pr.count(act_ready, CHUNKS), pr.count(weighted, CHUNKS)

            def copy_x():
                pr.read(M0)
                nc.scalar.copy(xn_rev[:], M0.ps[:, ::-1])
                nc.scalar.copy(xn_t[:], M0.ps[:]).then_inc(M0.free, 1)
                pr.skip(M0)

            def split_qk_hi():
                for w, b in enumerate((GATE, UP)):
                    pr.read(b)
                    nc.scalar.activation(qk_hi[:, w, :], b.ps[:], ACT.Identity, bias=cols[:, w:w + 1]).then_inc(qk_hi_done, 1)

            def router_exp():
                act.wait_ge(shifted_ready, shifted_n.step())
                nc.scalar.activation(exps[:], shifted[:].rearrange("p q e -> p (q e)"), ACT.Exp).then_inc(exps_ready, 1)

            def copy_combine():
                pr.read(M1)
                nc.scalar.mul(comb_scaled, M1.ps[0:EXPERTS, :], 1.0 / ALPHA)
                nc.scalar.copy(comb_t[:], M1.ps[0:EXPERTS, :]).then_inc(M1.free, 1)

            def gate_up(k):
                e, c = divmod(k, 2)
                n = act_n.step() - SU_SLOTS
                weighted_n.step()
                if not isinstance(n, int) or n > 0:
                    act.wait_ge(act_ready, n)
                    act.wait_ge(weighted, n)
                pr.read(GATE)
                col = 4 * e + c
                nc.scalar.activation(s_buf[:, k % SU_SLOTS, :], GATE.ps[:], ACT.Silu, bias=gate_bias[:, col:col + 1],
                                     scale=ALPHA).then_inc(GATE.free, 1)
                pr.read(UP)
                nc.scalar.activation(u_buf[:, k % SU_SLOTS, :], UP.ps[:], ACT.Identity,
                                     bias=up_bias[:, col + 2:col + 3]).then_inc(UP.free, 1)

            def negate_max(b):
                pr.read(M1)
                nc.scalar.activation(neg_max[:, b * SEQ:b * SEQ + SEQ], M1.ps[0:HEADS, 0:SEQ], ACT.Copy,
                                     scale=-1.0).then_inc(M1.free, 1)

            def exponents(u, pv_done):
                s = S[u % 2]
                if pv_done is not None:
                    act.wait_ge(PV.full, pv_done)
                pr.read(s)
                nc.scalar.activation(probs[:, u % P_SLOTS, :], s.ps[:, 0:384], ACT.Exp).then_inc(s.free, 1)

            def copy_heads(grp):
                b, g = divmod(grp, 4)
                pr.read(PV)
                nc.scalar.copy(heads_t[:, g, b * SEQ:b * SEQ + SEQ], PV.ps[:, 0:SEQ]).then_inc(PV.free, 1)

            def copy_attn(b):
                pr.read(M1)
                nc.scalar.copy(attn_t[:, b * SEQ:b * SEQ + SEQ], M1.ps[:, 0:SEQ]).then_inc(M1.free, 1)

            def copy_y():
                pr.read(Y)
                nc.scalar.activation(y_t[:], Y.ps[:], ACT.Identity, bias=cols[:, 2:3]).then_inc(Y.free, 1)

            pr.read(S[0])
            nc.scalar.mul(dist, S[0].ps[0:HEADS, 0:SPAN], SCALE).then_inc(S[0].free, 1)
            act.wait_ge(w_loaded["attn_w"], 16)
            nc.scalar.copy(wqk_hi[:], wqk).then_inc(attn_w_hi, 1)
            act.wait_ge(w_loaded["small"], 16 * 10)
            nc.scalar.mul(gate_bias[:], gu_bias[:], ALPHA)
            nc.scalar.add(up_bias[:], gu_bias[:], 1.0).then_inc(biases_ready, 1)
            nc.scalar.copy(ident_r[:], ident[:]).then_inc(ident_ready, 1)
            copy_x()
            for c in range(4):
                act.wait_ge(w_loaded["gu"], 16 * 8)
                nc.scalar.copy(gu_hi[:, 512 * c:512 * c + 512], gu_raw[:, 512 * c:512 * c + 512]).then_inc(gu_hi_done, 1)
            split_qk_hi()
            router_exp()
            copy_combine()
            for c in range(4, 8):
                nc.scalar.copy(gu_hi[:, 512 * c:512 * c + 512], gu_raw[:, 512 * c:512 * c + 512]).then_inc(gu_hi_done, 1)
            act.wait_ge(w_loaded["bias_raw"], 16)
            nc.scalar.copy(bias_hi[:, :, 0:256], bias_raw).then_inc(bias_hi_done, 1)
            nc.scalar.copy(bias_hi[:, :, 256:384], bias_raw[:, :, 0:128]).then_inc(bias_hi_done, 1)
            pr.skip(M1)
            act.wait_ge(biases_ready, 1)
            for k in range(LAG):
                gate_up(k)

            def body(t, last):
                pr.begin(t)
                for k in range(LAG, CHUNKS):
                    gate_up(k)
                    if k == 11:
                        negate_max(0)
                negate_max(1)
                for s in S:
                    pr.skip(s, 16)
                pv0 = pr.uses[id(PV)].now()
                for grp in range(8):
                    for u in range(4 * grp, 4 * grp + 4):
                        if grp == 0 and u == 0:
                            act.wait_ge(bias_split, 1)
                        exponents(u, pv0 + (grp - 1) if grp >= 2 else None)
                    if grp:
                        copy_heads(grp - 1)
                    if grp == 1 and not last:
                        copy_x()
                    if grp == 3 and not last:
                        split_qk_hi()
                    if grp == 4 and not last:
                        router_exp()
                    if grp == 6 and not last:
                        copy_combine()
                    if grp == 7:
                        copy_attn(0)
                copy_heads(7)
                if not last:
                    pr.skip(M1)
                    gate_up(0)
                    gate_up(1)
                copy_attn(1)
                if not last:
                    gate_up(2)
                copy_y()
                pr.skip(M0, 5)
                if not last:
                    gate_up(3)

            with act.Fori(0, N - 1) as t:
                body(t, False)
            body(N - 1, True)

        @block.vector
        def _(dve):
            pr = Program(dve)
            x_n, xres_n = pr.count(w_loaded["x"], 1, 16), pr.count(w_loaded["x_res"], 1, 16)
            rstd_n, exps_n = pr.count(rstd_ready, 1), pr.count(exps_ready, 1)
            qk_n = pr.count(qk_hi_done, 2)
            own = pr.count(dve_step, DVE_STEPS)

            def link(ins):
                ins.then_inc(dve_step, 1)
                pr.wait(dve_step, own.step())

            def normalise():
                dve.wait_ge(w_loaded["x"], x_n.step())
                for q in range(TILES):
                    i = nc.vector.bn_stats(stats[:, q, :], x_in[:, q, :])
                link(i)
                for q in range(TILES):
                    i = nc.vector.bn_aggr(mean_var[:, q, :], stats[:, q, :])
                link(i)
                nc.vector.tensor_scalar(var_eps[:], mean_var[:, :, 1], EPS, None, ALU.add).then_inc(var_ready, 1)
                dve.wait_ge(rstd_ready, rstd_n.step())
                for q in range(TILES):
                    i = nc.vector.tensor_scalar(xn[:, q, :], x_in[:, q, :], mean_var[:, q, 0:1], rstd[:, q:q + 1],
                                                ALU.subtract, ALU.mult)
                    if q == TILES - 1:
                        i.then_inc(xn_ready, 1)

            def split_x():
                dve.wait_ge(M0.free, pr.skip(M0))
                link(nc.vector.tensor_copy(xn_hi[:], xn_t[:]))
                nc.vector.tensor_tensor(xn_lo[:], xn_t[:], xn_hi[:].bitcast(F32), ALU.subtract).then_inc(xn_split, 1)

            def route():
                pr.read(M0)
                i = nc.vector.tensor_tensor(logits[:], M0.ps[:, 0:32].rearrange("p (q e) -> p q e", q=TILES),
                                            rb_rows[:].unsqueeze(1).broadcast_to([P, TILES, EXPERTS]), ALU.add)
                i.then_inc(M0.free, 1)
                dve.wait_ge(M0.free, pr.uses[id(M0)].now())
                link(nc.vector.tensor_reduce(top[:], logits[:], AX.X, ALU.max))
                nc.vector.tensor_tensor(shifted[:], logits[:], top[:].unsqueeze(2).broadcast_to([P, TILES, EXPERTS]),
                                        ALU.subtract).then_inc(shifted_ready, 1)
                four = [P, TILES, EXPERTS, EXPERTS]
                link(nc.vector.tensor_tensor(diff[:].rearrange("p (q i j) -> p q i j", q=TILES, i=EXPERTS),
                                             logits[:].unsqueeze(2).broadcast_to(four),
                                             logits[:].unsqueeze(3).broadcast_to(four), ALU.subtract))
                link(nc.vector.scalar_tensor_tensor(ahead[:], diff[:], 0.0, tri[:], ALU.is_ge, ALU.mult))
                link(nc.vector.scalar_tensor_tensor(ahead[:], diff[:], 0.0, ahead[:], ALU.is_gt, ALU.max))
                link(nc.vector.tensor_reduce(rank[:], ahead[:].rearrange("p (i j) -> p i j", j=EXPERTS), AX.X, ALU.add))
                dve.wait_ge(exps_ready, exps_n.step())
                link(nc.vector.scalar_tensor_tensor(kept[:], rank[:], float(TOP_K), exps[:], ALU.is_lt, ALU.mult))
                link(nc.vector.tensor_reduce(total[:], kept[:].rearrange("p (q e) -> p q e", q=TILES), AX.X, ALU.add))
                link(nc.vector.reciprocal(total_inv[:], total[:]))
                nc.vector.tensor_tensor(combine[:], kept[:].rearrange("p (q e) -> p q e", q=TILES),
                                        total_inv[:].unsqueeze(2).broadcast_to([P, TILES, EXPERTS]),
                                        ALU.mult).then_inc(combine_ready, 1)

            def split_qk_lo():
                for w, b in enumerate((GATE, UP)):
                    pr.skip(b)
                    dve.wait_ge(qk_hi_done, qk_n.step())
                    nc.vector.scalar_tensor_tensor(qk_lo[:, w, :], b.ps[:], cols[:, w:w + 1], qk_hi[:, w, :].bitcast(F32),
                                                   ALU.add, ALU.subtract).then_inc(b.free, 1)

            def copy_v():
                pr.read(M1)
                nc.vector.tensor_tensor(v_heads[:, :, :, 0:HD], M1.ps[:].rearrange("p (q h d) -> p q h d", q=TILES, h=HEADS),
                                        bv_rows[:].rearrange("p (h d) -> p h d", h=HEADS).unsqueeze(1).broadcast_to([P, TILES, HEADS, HD]),
                                        ALU.add).then_inc(M1.free, 1)

            def clip_up(k):
                dve.wait_ge(GATE.free, pr.skip(GATE))
                dve.wait_ge(UP.free, pr.skip(UP))
                u = u_buf[:, k % SU_SLOTS, :]
                nc.vector.tensor_scalar(u, u, LIMIT + 1.0, 1.0 - LIMIT, ALU.min, ALU.max).then_inc(dve_step, 1)
                return own.step()

            def activate(k, clipped):
                s, u = s_buf[:, k % SU_SLOTS, :], u_buf[:, k % SU_SLOTS, :]
                dve.wait_ge(dve_step, clipped)
                nc.vector.scalar_tensor_tensor(s, s, CLIP, u, ALU.min, ALU.mult).then_inc(act_ready, 1)

            def reduce_max(u, b, r, g):
                s, h = S[u % 2], 4 * r + g
                pr.read(s, apart=True)
                for qt, c0, c1 in ((0, 0, 128), (1, 128, 384)):
                    i = nc.vector.tensor_tensor_reduce(s.ps[:, c0:c1], s.ps[:, c0:c1], bias_hi[:, h, 0:c1 - c0].bitcast(F32), 1.0, -3.0e38,
                                                       ALU.add, ALU.max, row_max[:, 2 * b + qt, h:h + 1])
                i.then_inc(s.free, 1)

            def norm_heads(q):
                pr.read(M0)
                v = M0.ps[:].rearrange("p (g r w) -> p r g w", g=NG, r=4)
                link(nc.vector.reciprocal(recip[:, q, :].rearrange("p (r g) -> p r g", g=NG), v[:, :, :, HD]))
                nc.vector.tensor_tensor(attn[:, q, :].rearrange("p (r g d) -> p r g d", r=4, g=NG), v[:, :, :, 0:HD],
                                        recip[:, q, :].rearrange("p (r g) -> p r g", g=NG).unsqueeze(3).broadcast_to([P, 4, NG, HD]),
                                        ALU.mult).then_inc(M0.free, 1)

            def add_residual():
                pr.read(M0)
                dve.wait_ge(w_loaded["x_res"], xres_n.step())
                nc.vector.tensor_tensor(x_res[:].rearrange("p q c -> p (q c)"), M0.ps[:],
                                        x_res[:].rearrange("p q c -> p (q c)"), ALU.add).then_inc(M0.free, 1)

            def split_gu(c):
                dve.wait_ge(gu_hi_done, c + 1)
                w = slice(512 * c, 512 * c + 512)
                nc.vector.tensor_tensor(gu_lo[:, w], gu_raw[:, w], gu_hi[:, w].bitcast(F32), ALU.subtract).then_inc(gu_split, 1)

            dve.wait_ge(S[0].free, pr.skip(S[0]))
            nc.vector.memset(dist[:, 0:127], MASKED).then_inc(dist_ready, 1)
            normalise()
            dve.wait_ge(attn_w_hi, 1)
            nc.vector.tensor_tensor(wqk_lo[:], wqk, wqk_hi[:].bitcast(F32), ALU.subtract).then_inc(attn_w_split, 1)
            dve.wait_ge(w_loaded["small"], 16 * 10)
            split_x()
            route()
            split_qk_lo()
            dve.wait_ge(filled, 4)
            pr.skip(M1)
            copy_v()
            for c in range(8):
                split_gu(c)
            for k in range(LAG):
                activate(k, clip_up(k))
            dve.wait_ge(bias_hi_done, 2)

            def body(t, last):
                pr.begin(t)
                todo = units(0, 32)
                for k in range(LAG, CHUNKS):
                    clipped = clip_up(k)
                    for u in todo[:1]:
                        reduce_max(*u)
                    activate(k, clipped)
                    for u in todo[1:3]:
                        reduce_max(*u)
                    todo = todo[3:]
                for s in S:
                    pr.skip(s, 16)
                pr.skip(M1, 2)
                if not last:
                    normalise()
                    dve.wait_ge(UP.free, pr.uses[id(UP)].now())
                    split_x()
                    route()
                    split_qk_lo()
                norm_heads(0)
                norm_heads(1)
                if not last:
                    pr.skip(M1)
                    pr.skip(M1)
                    copy_v()
                    activate(0, clip_up(0))
                else:
                    pr.skip(M1)
                norm_heads(2)
                norm_heads(3)
                pr.skip(M1)
                if not last:
                    for k in range(1, LAG):
                        activate(k, clip_up(k))
                add_residual()
                return

            with dve.Fori(0, N - 1) as t:
                body(t, False)
                measured["dve"] = own.local
            body(N - 1, True)

        @block.gpsimd
        def _(pool):
            pr = Program(pool)
            var_n, row_n = pr.count(var_ready, 1), pr.count(comb_row_loaded, 1, 16)
            act_n, down_n = pr.count(act_ready, CHUNKS), pr.count(down_done, CHUNKS)
            all_n = pr.count(comb_all_ready, 1)

            def inverse_std():
                pool.wait_ge(var_ready, var_n.step())
                nc.gpsimd.tensor_tensor(rstd[:], var_eps[:], minus_half[:], ALU.pow).then_inc(rstd_ready, 1)

            def spread_combine():
                pr.wait(comb_row_loaded, row_n.step())
                for e in range(EXPERTS):
                    i = nc.gpsimd.partition_broadcast(comb_all[:, e, :], comb_all[0:1, e, :], P)
                i.then_inc(comb_all_ready, 1)
                pool.wait_ge(comb_all_ready, all_n.step())

            def weigh(k):
                pool.wait_ge(act_ready, act_n.step())
                n = down_n.step() - AW_SLOTS
                if not isinstance(n, int) or n > 0:
                    pool.wait_ge(down_done, n)
                nc.gpsimd.tensor_tensor(aw_buf[:, k % AW_SLOTS, :], s_buf[:, k % SU_SLOTS, :], comb_all[:, k // 2, :],
                                        ALU.mult).then_inc(weighted, 1)

            nc.gpsimd.memset(minus_half[:], -0.5).then_inc(pool_step, 1)
            pool.wait_ge(pool_step, 1)
            inverse_std()
            nc.gpsimd.memset(v_one[:], 0.0).then_inc(filled, 1)
            pool.wait_ge(filled, 1)
            nc.gpsimd.memset(v_heads[:, :, :, HD:HD + 1], 1.0).then_inc(filled, 1)
            nc.gpsimd.memset(q_rows[:].bitcast(F32), 0.0).then_inc(filled, 1)
            nc.gpsimd.memset(k_rows[:].bitcast(F32), 1.0).then_inc(filled, 1)
            pool.wait_ge(gu_split, 8)
            spread_combine()
            for k in range(LAG):
                weigh(k)
            pool.wait_ge(bias_hi_done, 2)
            nc.gpsimd.tensor_tensor(bias_lo[:, :, 0:256], bias_raw, bias_hi[:, :, 0:256].bitcast(F32), ALU.subtract)
            nc.gpsimd.tensor_tensor(bias_lo[:, :, 256:384], bias_raw[:, :, 0:128], bias_hi[:, :, 256:384].bitcast(F32),
                                    ALU.subtract).then_inc(bias_split, 1)

            def body(t, last):
                pr.begin(t)
                for k in range(LAG, CHUNKS):
                    weigh(k)
                if not last:
                    inverse_std()
                    spread_combine()
                    for k in range(LAG):
                        weigh(k)

            with pool.Fori(0, N - 1) as t:
                body(t, False)
            body(N - 1, True)


measured = {}


def distance_one_hots():
    n = np.arange(256)
    exact = BUCKETS // 2
    ratio = np.log(np.maximum(n, 1).astype(np.float32) / np.float32(exact)) / np.float32(math.log(MAX_DISTANCE / exact))
    large = np.minimum(exact + (ratio * np.float32(BUCKETS - exact)).astype(np.int32), BUCKETS - 1)
    bucket = np.where(n < exact, n, large)
    hot = np.zeros((BUCKETS, SPAN), np.float32)
    hot[bucket, 127 + n] = 1.0
    return hot


def kernel(**inputs):
    import concourse.bacc as bacc
    from concourse.bass_utils import run_bass_kernel_spmd

    a = {k.replace("L0_attn_", "").replace("L0_ffn_", ""): np.asarray(v) for k, v in inputs.items()}
    batch, seq, d = a["x"].shape

    def by_rows(w):
        return w.reshape(4, NG, HD, -1).transpose(0, 2, 1, 3).reshape(P, -1)

    arrays = {
        "x": a["x"].reshape(batch * seq, d),
        "wqk": np.stack([by_rows(a["Wq"]).T, by_rows(a["Wk"]).T], axis=1),
        "wv": a["Wv"].T,
        "wo_t": a["Wo"].T,
        "cols": np.stack([by_rows(a["bq"])[:, 0], by_rows(a["bk"])[:, 0], a["bo"]], axis=1),
        "bv": a["bv"],
        "rel": a["rel_emb"],
        "onehot": distance_one_hots(),
        "ident": np.eye(P, dtype=np.float32),
        "tri": np.tile(np.tril(np.ones((EXPERTS, EXPERTS), np.float32), -1).reshape(-1), TILES),
        "wr_t": a["router_weight"].T,
        "rb": a["router_bias"],
        "gu_t": a["gate_up_proj"].reshape(-1, d).T,
        "gu_bias": a["gate_up_proj_bias"].reshape(-1, P).T,
        "dn_t": a["down_proj"].reshape(EXPERTS, d, 2, P).transpose(3, 0, 2, 1).reshape(P, CHUNKS, d),
        "dn_bias": a["down_proj_bias"],
    }
    arrays = {k: np.ascontiguousarray(v) for k, v in arrays.items()}

    def build(steps):
        nc = bacc.Bacc("TRN2", target_bir_lowering=False, num_devices=1)
        ins = {k: nc.dram_tensor(f"in_{k}", v.shape, mybir.dt.from_np(v.dtype), kind="ExternalInput").ap()
               for k, v in arrays.items()}
        out = nc.dram_tensor("out_y", (batch * seq, d), F32, kind="ExternalOutput").ap()
        build_layer(nc, ins, out, steps)
        return nc

    nc = build({"dve": DVE_STEPS_PER_BODY})
    r = run_bass_kernel_spmd(nc, [{f"in_{k}": v for k, v in arrays.items()}], core_ids=[0])
    return r.results[0]["out_y"].reshape(batch, seq, d)


DVE_STEPS_PER_BODY = 16 + 2 + 1 + 8 + 4
```

```python
from contextlib import ExitStack
import math

import numpy as np

import concourse.bass as bass
from concourse import mybir

F32 = mybir.dt.float32
F32R = mybir.dt.float32r
ACT = mybir.ActivationFunctionType
ALU = mybir.AluOpType
AX = mybir.AxisListType

P = 128
HEADS, HD = 16, 8
NG = 4
BUCKETS, MAX_DISTANCE = 32, 128
SCALE = HD ** -0.5
EPS = 1e-5
EXPERTS, TOP_K, INTER = 8, 4, 256
ALPHA, LIMIT = 1.702, 7.0
CLIP = ALPHA * LIMIT / (1.0 + math.exp(-ALPHA * LIMIT))
MASKED = -1.0e30
SPAN = 384
SEQ = 256
T = 512
TILES = T // P
CHUNKS = EXPERTS * INTER // P
AHEAD = 4
LAG = 8
SU_SLOTS, AW_SLOTS, P_SLOTS = 4, 9, 12


class Count:

    def __init__(self, per, by=1):
        self.per, self.by, self.base, self.local, self.t = per, by, 0, 0, None

    def begin(self, t):
        if self.t is None:
            self.base = self.local
        else:
            assert self.local in (0, self.per), (self.local, self.per)
        self.t, self.local = t, 0

    def step(self, n=1):
        self.local += n
        return self.now()

    def now(self):
        if self.t is None:
            return self.local * self.by
        return self.t * (self.per * self.by) + (self.base + self.local) * self.by


def build_layer(nc, ins, out):
    ctx = ExitStack()
    with ctx:
        def sb(name, shape, dt=F32):
            return ctx.enter_context(nc.sbuf_tensor(name, shape, dt))

        def bank(name):
            return ctx.enter_context(nc.psum_tensor(name, [P, 512], F32))

        def sem(name):
            return ctx.enter_context(nc.semaphore(name))

        ident = sb("ident", [P, P])
        wqk_hi = sb("wqk_hi", [P, 2, P], F32R)
        wqk_lo = sb("wqk_lo", [P, 2, P], F32R)
        wv = sb("wv", [P, P])
        wo_t = sb("wo_t", [P, P])
        wr_t = sb("wr_t", [P, EXPERTS])
        gu_hi = sb("gu_hi", [P, 4096], F32R)
        gu_lo = sb("gu_lo", [P, 4096], F32R)
        dn_t = sb("dn_t", [P, CHUNKS, P])
        dn_bias = sb("dn_bias", [EXPERTS, P])
        gu_bias = sb("gu_bias", [P, 32])
        gate_bias = sb("gate_bias", [P, 32])
        up_bias = sb("up_bias", [P, 32])
        cols = sb("cols", [P, 3])
        bv_rows = sb("bv_rows", [P, P])
        rb_rows = sb("rb_rows", [P, EXPERTS])
        tri = sb("tri", [P, TILES * 64])
        rel = sb("rel", [BUCKETS, HEADS])
        bias = sb("bias", [P, HEADS, 384])
        minus_half = sb("minus_half", [P, TILES])
        x_in = sb("x_in", [P, TILES, P])
        x_res = sb("x_res", [P, TILES, P])
        stats = sb("stats", [P, TILES, 6])
        mean_var = sb("mean_var", [P, TILES, 2])
        var_eps = sb("var_eps", [P, TILES])
        rstd = sb("rstd", [P, TILES])
        xn = sb("xn", [P, TILES, P])
        attn_t = xn[:, :, :].rearrange("p q c -> p (q c)")
        xn_t = sb("xn_t", [P, T])
        y_t = xn_t
        xn_rev = sb("xn_rev", [P, T])
        xn_hi = sb("xn_hi", [P, T], F32R)
        xn_lo = sb("xn_lo", [P, T], F32R)
        qk = sb("qk", [P, 2, T])
        qk_hi = sb("qk_hi", [P, 2, T], F32R)
        qk_lo = sb("qk_lo", [P, 2, T], F32R)
        q_rows = sb("q_rows", [P, NG, T], F32R)
        k_rows = sb("k_rows", [P, NG, T], F32R)
        v_one = sb("v_one", [P, TILES, HEADS * (HD + 1) + 32])
        v_heads = v_one[:, :, 0:HEADS * (HD + 1)].rearrange("p q (h w) -> p q h w", h=HEADS)
        row_max = sb("row_max", [P, TILES, HEADS])
        neg_max = sb("neg_max", [HEADS, T])
        probs = sb("probs", [P, P_SLOTS, 384])
        heads_t = sb("heads_t", [P, NG, T])
        recip = sb("recip", [P, TILES, HEADS])
        attn = sb("attn", [P, TILES, P])
        logits = sb("logits", [P, TILES, EXPERTS])
        shifted = sb("shifted", [P, TILES, EXPERTS])
        exps = sb("exps", [P, TILES * EXPERTS])
        top = sb("top", [P, TILES])
        diff = sb("diff", [P, TILES * 64])
        ahead = sb("ahead", [P, TILES * 64])
        rank = sb("rank", [P, TILES * EXPERTS])
        kept = sb("kept", [P, TILES * EXPERTS])
        total = sb("total", [P, TILES])
        total_inv = sb("total_inv", [P, TILES])
        combine = sb("combine", [P, TILES, EXPERTS])
        comb_t = sb("comb_t", [EXPERTS, T])
        comb_scaled = neg_max[0:EXPERTS, :]
        comb_all = sb("comb_all", [P, EXPERTS, T])
        gu_raw = comb_all[:, :, :].rearrange("p e t -> p (e t)")
        s_buf = sb("s_buf", [P, SU_SLOTS, T])
        u_buf = sb("u_buf", [P, SU_SLOTS, T])
        aw_buf = sb("aw_buf", [P, AW_SLOTS, T])
        wqk = aw_buf[:, 0, 0:2 * P].rearrange("p (w c) -> p w c", w=2)
        onehot = aw_buf[0:BUCKETS, 1, 0:SPAN]
        dist = aw_buf[0:HEADS, 3, 0:SPAN]
        dist_dram = nc.dram_tensor("dist_dram", [HEADS, SPAN], F32, kind="Internal")

        class Bank:

            def __init__(self, name, per, start=0):
                self.ps, self.full, self.free = bank(name), sem(name + "_full"), sem(name + "_free")
                self.per, self.start = per, start

        GATE = Bank("gate", 1 + CHUNKS)
        UP = Bank("up", 1 + CHUNKS)
        S = [Bank("scores0", 32), Bank("scores1", 32, start=1)]
        PV = Bank("pv", 8, start=1)
        Y = Bank("y", 1, start=1)
        M0 = Bank("misc0", 7)
        M1 = Bank("misc1", 6)
        BANKS = [GATE, UP, *S, PV, Y, M0, M1]

        w_loaded = {n: sem(n + "_loaded") for n in ("attn_w", "small", "gu", "dn", "hot", "bias", "x", "x_res")}
        dist_ready, dist_stored = sem("dist_ready"), sem("dist_stored")
        filled = sem("filled")
        attn_w_hi, attn_w_split = sem("attn_w_hi"), sem("attn_w_split")
        gu_hi_done, gu_split = sem("gu_hi_done"), sem("gu_split")
        biases_ready = sem("biases_ready")
        var_ready, rstd_ready, xn_ready = sem("var_ready"), sem("rstd_ready"), sem("xn_ready")
        xn_split, xn_rev_ready, qk_split = sem("xn_split"), sem("xn_rev_ready"), sem("qk_split")
        rows_loaded, max_loaded = sem("rows_loaded"), [sem("max0_loaded"), sem("max1_loaded")]
        shifted_ready, exps_ready, combine_ready = sem("shifted_ready"), sem("exps_ready"), sem("combine_ready")
        comb_row_loaded, comb_all_ready = sem("comb_row_loaded"), sem("comb_all_ready")
        probs_ready = sem("probs_ready")
        act_ready, weighted, slot_free = sem("act_ready"), sem("weighted"), sem("slot_free")
        stored = sem("stored")
        dve_step, pool_step = sem("dve_step"), sem("pool_step")
        x_view = ins["x"].rearrange("(n q p) c -> n p q c", p=P, q=TILES)
        out_view = out.rearrange("(n q p) c -> n p q c", p=P, q=TILES)
        N = x_view.shape[0]

        def units(first, last):
            return [(u, u // 16, u % 4, u % 16 // 4) for u in range(first, last)]

        class Program:

            def __init__(self, eng):
                self.eng = eng
                self.uses = {id(b): Count(b.per) for b in BANKS}
                self.counts = {}
                self.value = None

            def count(self, s, per, by=1):
                return self.counts.setdefault(id(s), Count(per, by))

            def begin(self, t):
                for c in [*self.uses.values(), *self.counts.values()]:
                    c.begin(t)

            def wait(self, s, n):
                if not isinstance(n, int):
                    self.value = self.value or self.eng.alloc_register("awaited")
                    self.eng.reg_add(self.value, n, 0)
                    self.eng.wait_ge(dist_ready, 1)
                    n = self.value
                self.eng.wait_ge(s, n)

            def fill(self, b):
                n = self.uses[id(b)].step() - 1 + b.start
                if not isinstance(n, int) or n > 0:
                    self.eng.wait_ge(b.free, n)

            def released(self, b):
                return self.uses[id(b)].now() + b.start

            def read(self, b, apart=False):
                n = self.uses[id(b)].step()
                (self.wait if apart else self.eng.wait_ge)(b.full, n)

            def skip(self, b, n=1):
                return self.uses[id(b)].step(n)

        block = ctx.enter_context(nc.Block())

        @block.sync
        def _(sp):
            pr = Program(sp)
            xn_ready_n = pr.count(xn_ready, 1)
            stored_n = pr.count(stored, 1, 16)
            weighted_n, qk_split_n = pr.count(weighted, CHUNKS), pr.count(qk_split, 1, 2)
            small = [(ident[:], ins["ident"]), (cols[:], ins["cols"]), (wr_t[:], ins["wr_t"]),
                     (rb_rows[:], ins["rb"].partition_broadcast(P)), (bv_rows[:], ins["bv"].partition_broadcast(P)),
                     (tri[:], ins["tri"].partition_broadcast(P)), (dn_bias[:], ins["dn_bias"]),
                     (gu_bias[:], ins["gu_bias"]), (wo_t[:], ins["wo_t"]), (wv[:], ins["wv"])]
            sp.dma_start(x_in[:], x_view[0]).then_inc(w_loaded["x"], 16)
            sp.dma_start(rel[:], ins["rel"]).then_inc(w_loaded["hot"], 16)
            sp.dma_start(onehot, ins["onehot"]).then_inc(w_loaded["hot"], 16)
            sp.dma_start(wqk, ins["wqk"]).then_inc(w_loaded["attn_w"], 16)
            for dst, src in small:
                sp.dma_start(dst, src).then_inc(w_loaded["small"], 16)
            for c in range(8):
                sp.dma_start(gu_raw[:, 512 * c:512 * c + 512], ins["gu_t"][:, 512 * c:512 * c + 512]).then_inc(w_loaded["gu"], 16)
            sp.wait_ge(dist_ready, 1)
            sp.dma_start(dist_dram.ap(), dist).then_inc(dist_stored, 16)
            sp.wait_ge(dist_stored, 16)
            for c0, c1 in ((0, 256), (256, 384)):
                sp.dma_start(bias[:, :, c0:c1], bass.AP(dist_dram, 0, [[1, P], [SPAN, HEADS], [1, c1 - c0]])).then_inc(w_loaded["bias"], 16)
            sp.dma_start(dn_t[:], ins["dn_t"]).then_inc(w_loaded["dn"], 16)
            sp.dma_start(x_res[:], x_view[0]).then_inc(w_loaded["x_res"], 16)

            def load_comb_row():
                pr.wait(M1.free, pr.skip(M1))
                if pr.uses[id(M1)].t is not None:
                    pr.wait(weighted, weighted_n.now())
                else:
                    sp.wait_ge(gu_split, 8)
                sp.dma_start(comb_all[0:1, :, :], comb_scaled).then_inc(comb_row_loaded, 16)

            def load_rows():
                pr.wait(qk_split, qk_split_n.step())
                for rows, which, parts in ((q_rows, 0, (qk_hi, qk_hi, qk_lo)), (k_rows, 1, (qk_hi, qk_lo, qk_hi))):
                    for a, part in enumerate(parts):
                        sp.dma_start(rows[a:P:4].bitcast(F32), part[:, which, :].bitcast(F32)).then_inc(rows_loaded, 16)

            pr.skip(M1, 0)
            load_comb_row()
            sp.wait_ge(filled, 4)
            load_rows()
            pr.skip(M1)

            def body(t, last):
                pr.begin(t)
                if not last:
                    pr.wait(xn_ready, xn_ready_n.step())
                    sp.dma_start(x_in[:], x_view[t + 1]).then_inc(w_loaded["x"], 16)
                for b in range(2):
                    pr.wait(M1.free, pr.skip(M1))
                    sp.dma_start(q_rows[31:P:32, :, b * SEQ:b * SEQ + SEQ].bitcast(F32),
                                 neg_max[:, b * SEQ:b * SEQ + SEQ]).then_inc(max_loaded[b], 16)
                weighted_n.step(CHUNKS - AHEAD + 1)
                if not last:
                    load_comb_row()
                    weighted_n.step(AHEAD - 1)
                    for b in range(2):
                        pr.wait(S[b].full, pr.skip(S[b], 32))
                    load_rows()
                    pr.skip(M1)
                pr.skip(M1, 2)
                pr.wait(M0.free, pr.skip(M0, 7 if not last else 5))
                sp.dma_start(out_view[t], x_res[:]).then_inc(stored, 16)
                stored_n.step()
                pr.wait(stored, stored_n.now())
                if not last:
                    sp.dma_start(x_res[:], x_view[t + 1]).then_inc(w_loaded["x_res"], 16)

            pr.skip(M0, 2)
            weighted_n.step(AHEAD - 1)
            pr.skip(S[0])
            with sp.Fori(0, N - 1) as t:
                body(t, False)
            body(N - 1, True)

        @block.tensor
        def _(pe):
            pr = Program(pe)
            xn_ready_n, xn_split_n = pr.count(xn_ready, 1), pr.count(xn_split, 1)
            rows_n, max_n = pr.count(rows_loaded, 6, 16), [pr.count(m, 1, 16) for m in max_loaded]
            comb_n, weighted_n = pr.count(combine_ready, 1), pr.count(weighted, CHUNKS)
            probs_n, rev_n = pr.count(probs_ready, 16), pr.count(xn_rev_ready, 1)
            freed = {}

            def split_product(dst, hi, lo, rhs_hi, rhs_lo):
                nc.tensor.matmul(dst, lo, rhs_hi, start=True, stop=False)
                nc.tensor.matmul(dst, hi, rhs_lo, start=False, stop=False)
                return nc.tensor.matmul(dst, hi, rhs_hi, start=False, stop=True)

            def transpose_x():
                pr.fill(M0)
                pe.wait_ge(xn_ready, xn_ready_n.step())
                for q in range(TILES):
                    mm = nc.tensor.transpose(M0.ps[:, q * P:q * P + P], xn[:, q, :], ident[:])
                mm.then_inc(M0.full, 1)
                freed["xn_t"] = pr.released(M0)

            def router():
                pe.wait_ge(M0.free, freed["xn_t"])
                pr.fill(M0)
                for q in range(TILES):
                    mm = nc.tensor.matmul(M0.ps[:, q * EXPERTS:(q + 1) * EXPERTS], xn_t[:, q * P:q * P + P], wr_t[:],
                                          start=True, stop=True)
                mm.then_inc(M0.full, 1)

            def project_q():
                pe.wait_ge(xn_split, xn_split_n.step())
                pr.fill(GATE)
                split_product(GATE.ps[:], wqk_hi[:, 0, :], wqk_lo[:, 0, :], xn_hi[:], xn_lo[:]).then_inc(GATE.full, 1)

            def project_k():
                pr.fill(UP)
                split_product(UP.ps[:], wqk_hi[:, 1, :], wqk_lo[:, 1, :], xn_hi[:, ::-1], xn_lo[:, ::-1]).then_inc(UP.full, 1)

            def project_v():
                pr.fill(M1)
                pe.wait_ge(xn_rev_ready, rev_n.step())
                for q in range(TILES):
                    mm = nc.tensor.matmul(M1.ps[:, q * P:q * P + P], xn_rev[:, q * P:q * P + P], wv[:], start=True, stop=True)
                mm.then_inc(M1.full, 1)

            def transpose_combine():
                pr.fill(M1)
                pe.wait_ge(combine_ready, comb_n.step())
                for q in range(TILES):
                    mm = nc.tensor.transpose(M1.ps[0:EXPERTS, q * P:q * P + P], combine[:, q, :], ident[:])
                mm.then_inc(M1.full, 1)

            def gate_up_half(k, half):
                b, (e, c) = (GATE, UP)[half], divmod(k, 2)
                w = slice(e * 512 + half * 256 + c * P, e * 512 + half * 256 + c * P + P)
                pr.fill(b)
                split_product(b.ps[:], gu_hi[:, w], gu_lo[:, w], xn_hi[:], xn_lo[:]).then_inc(b.full, 1)

            def gate_up(k):
                gate_up_half(k, 0)
                gate_up_half(k, 1)

            def down(k):
                if k == 0:
                    pr.fill(Y)
                    nc.tensor.matmul(Y.ps[:], dn_bias[:], comb_t[:], start=True, stop=False)
                pe.wait_ge(weighted, weighted_n.step())
                nc.tensor.matmul(Y.ps[:], dn_t[:, k, :], aw_buf[:, k % AW_SLOTS, :], start=False, stop=False).then_inc(slot_free, 1)

            def max_scores(u, b, r, g):
                s = S[u % 2]
                pr.fill(s)
                rows = slice(32 * r, 32 * r + 31)
                q, k = q_rows[rows, g, b * SEQ:(b + 1) * SEQ], k_rows[rows, g, (1 - b) * SEQ:(2 - b) * SEQ]
                nc.tensor.matmul(s.ps[:, 0:P], q[:, 0:P], k[:, P:SEQ], start=True, stop=True)
                mm = nc.tensor.matmul(s.ps[:, P:P + SEQ], q[:, P:SEQ], k, start=True, stop=True)
                mm.then_inc(s.full, 1)
                freed["max", b, u % 2] = pr.released(s)

            def transpose_max(b):
                for s in S:
                    pe.wait_ge(s.free, freed["max", b, s is S[1]])
                pr.fill(M1)
                for q in range(2):
                    mm = nc.tensor.transpose(M1.ps[0:HEADS, q * P:q * P + P], row_max[:, 2 * b + q, :], ident[:])
                mm.then_inc(M1.full, 1)

            def prob_scores(u, b, r, g):
                s = S[u % 2]
                pr.fill(s)
                rows = slice(32 * r, 32 * r + 32)
                q, k = q_rows[rows, g, b * SEQ:(b + 1) * SEQ], k_rows[rows, g, (1 - b) * SEQ:(2 - b) * SEQ]
                nc.tensor.matmul(s.ps[:, 0:SEQ], k[:, P:SEQ], q, start=True, stop=True)
                nc.tensor.matmul(s.ps[:, SEQ:SEQ + P], k[:, 0:P], q[:, P:SEQ], start=True, stop=True).then_inc(s.full, 1)

            def weigh_values(grp, kt):
                b, g = divmod(grp, 4)
                if kt == 0:
                    pr.fill(PV)
                    pe.wait_ge(probs_ready, probs_n.step(2))
                for r in range(4):
                    h, p = 4 * r + g, probs[:, (4 * grp + r) % P_SLOTS, :]
                    mm = nc.tensor.matmul(PV.ps[32 * r:32 * r + 32, kt * P:256],
                                          v_one[:, 2 * (1 - b) + 1 - kt, h * (HD + 1):h * (HD + 1) + 32],
                                          p[:, 256 * kt:256 + 128 * kt],
                                          start=(kt == 0), stop=(kt == 1), tile_position=(0, 32 * r))
                if kt == 1:
                    mm.then_inc(PV.full, 1)
                    freed["heads", grp] = pr.released(PV)

            def transpose_heads(q):
                pr.fill(M0)
                pe.wait_ge(PV.free, freed["heads", 4 * (q // 2) + 3])
                for g in range(NG):
                    mm = nc.tensor.transpose(M0.ps[:, g * P:g * P + P], heads_t[:, g, q * P:q * P + P], ident[:])
                mm.then_inc(M0.full, 1)
                freed["norm", q] = pr.released(M0)

            def transpose_attn(b):
                pe.wait_ge(M0.free, freed["norm", 2 * b + 1])
                pr.fill(M1)
                for q in range(2):
                    mm = nc.tensor.transpose(M1.ps[:, q * P:q * P + P], attn[:, 2 * b + q, :], ident[:])
                mm.then_inc(M1.full, 1)
                freed["attn_t", b] = pr.released(M1)

            def project_out():
                pe.wait_ge(M1.free, freed["attn_t", 1])
                nc.tensor.matmul(Y.ps[:], wo_t[:], attn_t, start=False, stop=True).then_inc(Y.full, 1)

            def transpose_y():
                pr.fill(M0)
                pe.wait_ge(Y.free, pr.released(Y))
                for q in range(TILES):
                    mm = nc.tensor.transpose(M0.ps[:, q * P:q * P + P], y_t[:, q * P:q * P + P], ident[:])
                mm.then_inc(M0.full, 1)

            pe.wait_ge(w_loaded["hot"], 32)
            pr.fill(S[0])
            nc.tensor.matmul(S[0].ps[0:HEADS, 0:SPAN], rel[:], onehot, start=True, stop=True).then_inc(S[0].full, 1)
            for i, (semaphore, n) in enumerate(((S[1].free, 1), (Y.free, 1), (slot_free, AW_SLOTS), (PV.free, 1))):
                nc.tensor.matmul(PV.ps[0:HEADS, 4 * i:4 * i + 4], rel[:], onehot[:, 0:4], start=True, stop=True).then_inc(semaphore, n)
            pe.wait_ge(w_loaded["small"], 16 * 10)
            transpose_x()
            pe.wait_ge(attn_w_split, 1)
            router()
            project_q()
            project_k()
            transpose_combine()
            project_v()
            for k in range(AHEAD):
                if k % 2 == 0:
                    pe.wait_ge(gu_split, k // 2 + 1)
                gate_up(k)

            def body(t, last):
                pr.begin(t)
                todo = units(0, 32)
                pe.wait_ge(rows_loaded, rows_n.step(6))
                for k in range(AHEAD, CHUNKS):
                    if k % 2 == 0:
                        pe.wait_ge(gu_split, k // 2 + 1)
                    scores = todo[:3]
                    todo = todo[3:]
                    if scores:
                        max_scores(*scores[0])
                    gate_up_half(k, 0)
                    if len(scores) > 1:
                        max_scores(*scores[1])
                    gate_up_half(k, 1)
                    if len(scores) > 2:
                        max_scores(*scores[2])
                    if k == 10:
                        transpose_max(0)
                    if k == LAG:
                        pe.wait_ge(w_loaded["dn"], 16)
                    if k >= LAG:
                        down(k - LAG)
                assert not todo
                if not last:
                    transpose_x()
                late = iter(range(CHUNKS - LAG, CHUNKS))
                down(next(late))
                transpose_max(1)
                for grp in range(8):
                    if grp % 4 == 0:
                        pe.wait_ge(max_loaded[grp // 4], max_n[grp // 4].step())
                    first, second = units(4 * grp, 4 * grp + 2), units(4 * grp + 2, 4 * grp + 4)
                    for u in first:
                        prob_scores(*u)
                    if grp >= 2:
                        weigh_values(grp - 2, 1)
                    if grp in (0, 1, 3, 4):
                        down(next(late))
                    if not last:
                        if grp == 2:
                            project_q()
                        if grp == 5:
                            transpose_combine()
                        if grp == 7:
                            gate_up_half(0, 1)
                    for u in second:
                        prob_scores(*u)
                    if grp >= 1:
                        weigh_values(grp - 1, 0)
                    if grp == 0:
                        down(next(late))
                    if grp == 5:
                        transpose_heads(0)
                    if grp == 6:
                        transpose_heads(1)
                    if not last:
                        if grp == 1:
                            router()
                        if grp == 2:
                            project_k()
                        if grp == 4:
                            gate_up_half(0, 0)
                weigh_values(6, 1)
                if not last:
                    project_v()
                weigh_values(7, 0)
                weigh_values(7, 1)
                down(next(late))
                transpose_heads(2)
                down(next(late))
                transpose_attn(0)
                transpose_heads(3)
                if not last:
                    gate_up(1)
                transpose_attn(1)
                if not last:
                    gate_up(2)
                for k in late:
                    down(k)
                project_out()
                if not last:
                    gate_up(3)
                transpose_y()

            with pe.Fori(0, N - 1) as t:
                body(t, False)
            body(N - 1, True)

        @block.scalar
        def _(act):
            pr = Program(act)
            shifted_n = pr.count(shifted_ready, 1)
            act_n, weighted_n = pr.count(act_ready, CHUNKS), pr.count(weighted, CHUNKS)

            def copy_x():
                pr.read(M0)
                nc.scalar.copy(xn_t[:], M0.ps[:])
                nc.scalar.copy(xn_hi[:], M0.ps[:]).then_inc(M0.free, 1)
                pr.skip(M0)

            def copy_qk():
                for w, b in enumerate((GATE, UP)):
                    pr.read(b)
                    nc.scalar.activation(qk[:, w, :], b.ps[:], ACT.Identity, bias=cols[:, w:w + 1])
                    nc.scalar.activation(qk_hi[:, w, :], b.ps[:], ACT.Identity, bias=cols[:, w:w + 1]).then_inc(b.free, 1)

            def router_exp():
                act.wait_ge(shifted_ready, shifted_n.step())
                nc.scalar.activation(exps[:], shifted[:].rearrange("p q e -> p (q e)"), ACT.Exp).then_inc(exps_ready, 1)

            def copy_combine():
                pr.read(M1)
                nc.scalar.mul(comb_scaled, M1.ps[0:EXPERTS, :], 1.0 / ALPHA)
                nc.scalar.copy(comb_t[:], M1.ps[0:EXPERTS, :]).then_inc(M1.free, 1)

            def gate_half(k):
                n = act_n.step() - SU_SLOTS
                weighted_n.step()
                if not isinstance(n, int) or n > 0:
                    act.wait_ge(act_ready, n)
                    act.wait_ge(weighted, n)
                pr.read(GATE)
                col = 4 * (k // 2) + k % 2
                nc.scalar.activation(s_buf[:, k % SU_SLOTS, :], GATE.ps[:], ACT.Silu, bias=gate_bias[:, col:col + 1],
                                     scale=ALPHA).then_inc(GATE.free, 1)

            def up_half(k):
                col = 4 * (k // 2) + k % 2
                pr.read(UP)
                nc.scalar.activation(u_buf[:, k % SU_SLOTS, :], UP.ps[:], ACT.Identity,
                                     bias=up_bias[:, col + 2:col + 3]).then_inc(UP.free, 1)

            def gate_up(k):
                gate_half(k)
                up_half(k)

            def negate_max(b):
                pr.read(M1)
                nc.scalar.activation(neg_max[:, b * SEQ:b * SEQ + SEQ], M1.ps[0:HEADS, 0:SEQ], ACT.Copy,
                                     scale=-1.0).then_inc(M1.free, 1)

            def exponents(u):
                for s in S:
                    pr.skip(s)
                    act.wait_ge(s.free, pr.released(s))
                p = probs[:, u % P_SLOTS:u % P_SLOTS + 2, :]
                nc.scalar.activation(p, p, ACT.Exp).then_inc(probs_ready, 1)

            def copy_heads(grp):
                b, g = divmod(grp, 4)
                pr.read(PV)
                nc.scalar.copy(heads_t[:, g, b * SEQ:b * SEQ + SEQ], PV.ps[:, 0:SEQ]).then_inc(PV.free, 1)

            def copy_attn(b):
                pr.read(M1)
                nc.scalar.copy(attn_t[:, b * SEQ:b * SEQ + SEQ], M1.ps[:, 0:SEQ]).then_inc(M1.free, 1)

            def copy_y():
                pr.read(Y)
                nc.scalar.activation(y_t[:], Y.ps[:], ACT.Identity, bias=cols[:, 2:3]).then_inc(Y.free, 1)

            pr.read(S[0])
            nc.scalar.mul(dist, S[0].ps[0:HEADS, 0:SPAN], SCALE).then_inc(S[0].free, 1)
            act.wait_ge(w_loaded["attn_w"], 16)
            nc.scalar.copy(wqk_hi[:], wqk).then_inc(attn_w_hi, 1)
            act.wait_ge(w_loaded["small"], 16 * 10)
            nc.scalar.mul(gate_bias[:], gu_bias[:], ALPHA)
            nc.scalar.add(up_bias[:], gu_bias[:], 1.0).then_inc(biases_ready, 1)
            copy_x()
            for c in range(4):
                act.wait_ge(w_loaded["gu"], 16 * 8)
                nc.scalar.copy(gu_hi[:, 512 * c:512 * c + 512], gu_raw[:, 512 * c:512 * c + 512]).then_inc(gu_hi_done, 1)
            copy_qk()
            router_exp()
            copy_combine()
            for c in range(4, 8):
                nc.scalar.copy(gu_hi[:, 512 * c:512 * c + 512], gu_raw[:, 512 * c:512 * c + 512]).then_inc(gu_hi_done, 1)
            pr.skip(M1)
            act.wait_ge(biases_ready, 1)
            for k in range(AHEAD):
                gate_up(k)

            def body(t, last):
                pr.begin(t)
                for k in range(AHEAD, CHUNKS):
                    gate_up(k)
                    if k == 11:
                        negate_max(0)
                if not last:
                    copy_x()
                negate_max(1)
                for s in S:
                    pr.skip(s, 16)
                for grp in range(8):
                    for u in (4 * grp, 4 * grp + 2):
                        exponents(u)
                    if grp:
                        copy_heads(grp - 1)
                    if grp == 2 and not last:
                        copy_qk()
                    if grp == 3 and not last:
                        router_exp()
                    if grp == 5 and not last:
                        copy_combine()
                copy_heads(7)
                if not last:
                    pr.skip(M1)
                    gate_up(0)
                copy_attn(0)
                if not last:
                    gate_up(1)
                copy_attn(1)
                if not last:
                    gate_up(2)
                copy_y()
                pr.skip(M0, 5)
                if not last:
                    gate_up(3)

            with act.Fori(0, N - 1) as t:
                body(t, False)
            body(N - 1, True)

        @block.vector
        def _(dve):
            pr = Program(dve)
            x_n, xres_n = pr.count(w_loaded["x"], 1, 16), pr.count(w_loaded["x_res"], 1, 16)
            rstd_n, exps_n = pr.count(rstd_ready, 1), pr.count(exps_ready, 1)
            own, pv_n = pr.count(dve_step, CHUNKS + 14), pr.count(PV.full, 8)
            done = {}

            def gives(name, ins):
                ins.then_inc(dve_step, 1)
                done[name] = own.step()

            def needs(name):
                dve.wait_ge(dve_step, done[name])

            def row_stats():
                dve.wait_ge(w_loaded["x"], x_n.step())
                for q in range(TILES):
                    i = nc.vector.bn_stats(stats[:, q, :], x_in[:, q, :])
                gives("stats", i)

            def mean_variance():
                pr.wait(dve_step, done["stats"])
                for q in range(TILES):
                    i = nc.vector.bn_aggr(mean_var[:, q, :], stats[:, q, :])
                gives("mean_var", i)

            def add_eps():
                needs("mean_var")
                nc.vector.tensor_scalar(var_eps[:], mean_var[:, :, 1], EPS, None, ALU.add).then_inc(var_ready, 1)

            def normalise():
                dve.wait_ge(rstd_ready, rstd_n.step())
                for q in range(TILES):
                    i = nc.vector.tensor_scalar(xn[:, q, :], x_in[:, q, :], mean_var[:, q, 0:1], rstd[:, q:q + 1],
                                                ALU.subtract, ALU.mult)
                i.then_inc(xn_ready, 1)

            def add_router_bias():
                pr.read(M0)
                nc.vector.tensor_tensor(logits[:], M0.ps[:, 0:32].rearrange("p (q e) -> p q e", q=TILES),
                                        rb_rows[:].unsqueeze(1).broadcast_to([P, TILES, EXPERTS]), ALU.add).then_inc(M0.free, 1)
                done["logits"] = pr.released(M0)

            def largest_logit():
                dve.wait_ge(M0.free, done["logits"])
                gives("top", nc.vector.tensor_reduce(top[:], logits[:], AX.X, ALU.max))

            def compare_logits():
                four = [P, TILES, EXPERTS, EXPERTS]
                gives("diff", nc.vector.tensor_tensor(diff[:].rearrange("p (q i j) -> p q i j", q=TILES, i=EXPERTS),
                                                      logits[:].unsqueeze(2).broadcast_to(four),
                                                      logits[:].unsqueeze(3).broadcast_to(four), ALU.subtract))

            def shift_logits():
                needs("top")
                nc.vector.tensor_tensor(shifted[:], logits[:], top[:].unsqueeze(2).broadcast_to([P, TILES, EXPERTS]),
                                        ALU.subtract).then_inc(shifted_ready, 1)

            def equal_or_greater():
                needs("diff")
                gives("ties", nc.vector.scalar_tensor_tensor(ahead[:], diff[:], 0.0, tri[:], ALU.is_ge, ALU.mult))

            def greater():
                needs("ties")
                gives("ahead", nc.vector.scalar_tensor_tensor(ahead[:], diff[:], 0.0, ahead[:], ALU.is_gt, ALU.max))

            def count_ahead():
                needs("ahead")
                gives("rank", nc.vector.tensor_reduce(rank[:], ahead[:].rearrange("p (i j) -> p i j", j=EXPERTS), AX.X, ALU.add))

            def keep_top():
                needs("rank")
                dve.wait_ge(exps_ready, exps_n.step())
                gives("kept", nc.vector.scalar_tensor_tensor(kept[:], rank[:], float(TOP_K), exps[:], ALU.is_lt, ALU.mult))

            def sum_kept():
                needs("kept")
                gives("total", nc.vector.tensor_reduce(total[:], kept[:].rearrange("p (q e) -> p q e", q=TILES), AX.X, ALU.add))

            def invert_total():
                needs("total")
                gives("total_inv", nc.vector.reciprocal(total_inv[:], total[:]))

            def combine_weights():
                needs("total_inv")
                nc.vector.tensor_tensor(combine[:], kept[:].rearrange("p (q e) -> p q e", q=TILES),
                                        total_inv[:].unsqueeze(2).broadcast_to([P, TILES, EXPERTS]),
                                        ALU.mult).then_inc(combine_ready, 1)

            def copy_v():
                pr.read(M1)
                nc.vector.tensor_tensor(v_heads[:, :, :, 0:HD], M1.ps[:].rearrange("p (q h d) -> p q h d", q=TILES, h=HEADS),
                                        bv_rows[:].rearrange("p (h d) -> p h d", h=HEADS).unsqueeze(1).broadcast_to([P, TILES, HEADS, HD]),
                                        ALU.add).then_inc(M1.free, 1)

            def clip_up(k):
                dve.wait_ge(GATE.free, pr.skip(GATE))
                dve.wait_ge(UP.free, pr.skip(UP))
                u = u_buf[:, k % SU_SLOTS, :]
                gives("clipped", nc.vector.tensor_scalar(u, u, LIMIT + 1.0, 1.0 - LIMIT, ALU.min, ALU.max))

            def activate(k):
                s, u = s_buf[:, k % SU_SLOTS, :], u_buf[:, k % SU_SLOTS, :]
                needs("clipped")
                nc.vector.scalar_tensor_tensor(s, s, CLIP, u, ALU.min, ALU.mult).then_inc(act_ready, 1)

            def reduce_max(u, b, r, g):
                s, h = S[u % 2], 4 * r + g
                pr.read(s, apart=True)
                for qt, c0, c1 in ((0, 0, 128), (1, 128, 384)):
                    i = nc.vector.tensor_tensor_reduce(s.ps[:, c0:c1], s.ps[:, c0:c1], bias[:, h, 0:c1 - c0], 1.0, -3.0e38,
                                                       ALU.add, ALU.max, row_max[:, 2 * b + qt, h:h + 1])
                i.then_inc(s.free, 1)

            def add_bias(u, b, r, g):
                s, h = S[u % 2], 4 * r + g
                if u >= P_SLOTS and u % 4 == 0:
                    dve.wait_ge(PV.full, pv_n.step())
                pr.read(s)
                nc.vector.tensor_tensor(probs[:, u % P_SLOTS, :], s.ps[:, 0:384], bias[:, h, :], ALU.add).then_inc(s.free, 1)

            def norm_heads(q):
                pr.read(M0)
                v = M0.ps[:].rearrange("p (g r w) -> p r g w", g=NG, r=4)
                gives("recip", nc.vector.reciprocal(recip[:, q, :].rearrange("p (r g) -> p r g", g=NG), v[:, :, :, HD]))
                needs("recip")
                nc.vector.tensor_tensor(attn[:, q, :].rearrange("p (r g d) -> p r g d", r=4, g=NG), v[:, :, :, 0:HD],
                                        recip[:, q, :].rearrange("p (r g) -> p r g", g=NG).unsqueeze(3).broadcast_to([P, 4, NG, HD]),
                                        ALU.mult).then_inc(M0.free, 1)

            def add_residual():
                pr.read(M0)
                dve.wait_ge(w_loaded["x_res"], xres_n.step())
                nc.vector.tensor_tensor(x_res[:].rearrange("p q c -> p (q c)"), M0.ps[:],
                                        x_res[:].rearrange("p q c -> p (q c)"), ALU.add).then_inc(M0.free, 1)

            def split_gu(c):
                dve.wait_ge(gu_hi_done, c + 1)
                w = slice(512 * c, 512 * c + 512)
                nc.vector.tensor_tensor(gu_lo[:, w], gu_raw[:, w], gu_hi[:, w].bitcast(F32), ALU.subtract).then_inc(gu_split, 1)

            def route():
                add_router_bias()
                largest_logit()
                compare_logits()
                shift_logits()
                equal_or_greater()
                greater()
                count_ahead()
                keep_top()
                sum_kept()
                invert_total()
                combine_weights()

            dve.wait_ge(S[0].free, pr.skip(S[0]))
            nc.vector.memset(dist[:, 0:127], MASKED).then_inc(dist_ready, 1)
            row_stats()
            mean_variance()
            add_eps()
            normalise()
            dve.wait_ge(attn_w_hi, 1)
            nc.vector.tensor_tensor(wqk_lo[:], wqk, wqk_hi[:].bitcast(F32), ALU.subtract).then_inc(attn_w_split, 1)
            dve.wait_ge(w_loaded["small"], 16 * 10)
            pr.skip(M0)
            pr.skip(GATE)
            pr.skip(UP)
            route()
            dve.wait_ge(filled, 4)
            pr.skip(M1)
            copy_v()
            for c in range(8):
                split_gu(c)
            for k in range(AHEAD - 1):
                clip_up(k)
                activate(k)
            dve.wait_ge(w_loaded["bias"], 32)

            def body(t, last):
                pr.begin(t)
                todo = units(0, 32)
                for k in range(AHEAD, CHUNKS):
                    scores = todo[:3]
                    todo = todo[3:]
                    if scores:
                        reduce_max(*scores[0])
                    clip_up(k - 1)
                    if len(scores) > 1:
                        reduce_max(*scores[1])
                    activate(k - 1)
                    if len(scores) > 2:
                        reduce_max(*scores[2])
                    if not last:
                        if k == 11:
                            row_stats()
                        if k == 12:
                            mean_variance()
                        if k == 13:
                            add_eps()
                        if k == 14:
                            normalise()
                clip_up(CHUNKS - 1)
                activate(CHUNKS - 1)
                pr.skip(M1, 2)
                for u, b, r, g in units(0, 32):
                    add_bias(u, b, r, g)
                    if not last:
                        if u == 0:
                            pr.skip(M0)
                            pr.skip(GATE)
                            pr.skip(UP)
                        if u == 8:
                            add_router_bias()
                        if u == 9:
                            largest_logit()
                            compare_logits()
                        if u == 10:
                            shift_logits()
                            equal_or_greater()
                        if u == 11:
                            greater()
                        if u == 12:
                            count_ahead()
                        if u == 17:
                            keep_top()
                        if u == 18:
                            sum_kept()
                        if u == 19:
                            invert_total()
                        if u == 20:
                            combine_weights()
                    if u == 25:
                        norm_heads(0)
                    if u == 29:
                        norm_heads(1)
                pv_done = pv_n.step(P_SLOTS // 4)
                if not last:
                    pr.skip(M1)
                    dve.wait_ge(PV.full, pv_done)
                    copy_v()
                pr.skip(M1, 2)
                norm_heads(2)
                if not last:
                    clip_up(0)
                    activate(0)
                norm_heads(3)
                if not last:
                    clip_up(1)
                    activate(1)
                    clip_up(2)
                    activate(2)
                add_residual()

            with dve.Fori(0, N - 1) as t:
                body(t, False)
            body(N - 1, True)

        @block.gpsimd
        def _(pool):
            pr = Program(pool)
            var_n, row_n = pr.count(var_ready, 1), pr.count(comb_row_loaded, 1, 16)
            act_n, free_n = pr.count(act_ready, CHUNKS), pr.count(slot_free, CHUNKS)
            all_n = pr.count(comb_all_ready, 1)

            def inverse_std():
                pool.wait_ge(var_ready, var_n.step())
                nc.gpsimd.tensor_tensor(rstd[:], var_eps[:], minus_half[:], ALU.pow).then_inc(rstd_ready, 1)

            def split_x():
                pool.wait_ge(M0.free, pr.skip(M0))
                nc.gpsimd.tensor_tensor(xn_lo[:], xn_t[:], xn_hi[:].bitcast(F32), ALU.subtract).then_inc(xn_split, 1)

            def reverse_x():
                nc.gpsimd.tensor_copy(xn_rev[:], xn_t[:, ::-1]).then_inc(xn_rev_ready, 1)

            def split_qk():
                for w, b in enumerate((GATE, UP)):
                    pool.wait_ge(b.free, pr.skip(b))
                    nc.gpsimd.tensor_tensor(qk_lo[:, w, :], qk[:, w, :], qk_hi[:, w, :].bitcast(F32),
                                            ALU.subtract).then_inc(qk_split, 1)

            def spread_combine():
                pr.wait(comb_row_loaded, row_n.step())
                for e in range(EXPERTS):
                    i = nc.gpsimd.partition_broadcast(comb_all[:, e, :], comb_all[0:1, e, :], P)
                i.then_inc(comb_all_ready, 1)
                pool.wait_ge(comb_all_ready, all_n.step())

            def weigh(k):
                pool.wait_ge(act_ready, act_n.step())
                pool.wait_ge(slot_free, free_n.step())
                nc.gpsimd.tensor_tensor(aw_buf[:, k % AW_SLOTS, :], s_buf[:, k % SU_SLOTS, :], comb_all[:, k // 2, :],
                                        ALU.mult).then_inc(weighted, 1)

            nc.gpsimd.memset(minus_half[:], -0.5).then_inc(pool_step, 1)
            pool.wait_ge(pool_step, 1)
            inverse_std()
            nc.gpsimd.memset(v_one[:], 0.0).then_inc(filled, 1)
            pool.wait_ge(filled, 1)
            nc.gpsimd.memset(v_heads[:, :, :, HD:HD + 1], 1.0).then_inc(filled, 1)
            nc.gpsimd.memset(q_rows[:].bitcast(F32), 0.0).then_inc(filled, 1)
            nc.gpsimd.memset(k_rows[:].bitcast(F32), 1.0).then_inc(filled, 1)
            split_x()
            reverse_x()
            split_qk()
            pool.wait_ge(gu_split, 8)
            spread_combine()
            for k in range(AHEAD - 1):
                weigh(k)

            pr.skip(M0)
            pr.skip(GATE, AHEAD)
            pr.skip(UP, AHEAD)

            def body(t, last):
                pr.begin(t)
                for k in range(AHEAD - 1, CHUNKS):
                    if k == 12 and not last:
                        inverse_std()
                    weigh(k)
                pr.skip(GATE, CHUNKS - AHEAD)
                pr.skip(UP, CHUNKS - AHEAD)
                if not last:
                    split_x()
                    split_qk()
                    reverse_x()
                    spread_combine()
                    pr.skip(M0, 6)
                    pr.skip(GATE, AHEAD)
                    pr.skip(UP, AHEAD)
                    for k in range(AHEAD - 1):
                        weigh(k)

            with pool.Fori(0, N - 1) as t:
                body(t, False)
            body(N - 1, True)


def distance_one_hots():
    n = np.arange(256)
    exact = BUCKETS // 2
    ratio = np.log(np.maximum(n, 1).astype(np.float32) / np.float32(exact)) / np.float32(math.log(MAX_DISTANCE / exact))
    large = np.minimum(exact + (ratio * np.float32(BUCKETS - exact)).astype(np.int32), BUCKETS - 1)
    bucket = np.where(n < exact, n, large)
    hot = np.zeros((BUCKETS, SPAN), np.float32)
    hot[bucket, 127 + n] = 1.0
    return hot


def kernel(**inputs):
    import concourse.bacc as bacc
    from concourse.bass_utils import run_bass_kernel_spmd

    a = {k.replace("L0_attn_", "").replace("L0_ffn_", ""): np.asarray(v) for k, v in inputs.items()}
    batch, seq, d = a["x"].shape

    def by_rows(w):
        return w.reshape(4, NG, HD, -1).transpose(0, 2, 1, 3).reshape(P, -1)

    arrays = {
        "x": a["x"].reshape(batch * seq, d),
        "wqk": np.stack([by_rows(a["Wq"]).T, by_rows(a["Wk"]).T], axis=1),
        "wv": a["Wv"].T,
        "wo_t": a["Wo"].T,
        "cols": np.stack([by_rows(a["bq"])[:, 0], by_rows(a["bk"])[:, 0], a["bo"]], axis=1),
        "bv": a["bv"],
        "rel": a["rel_emb"],
        "onehot": distance_one_hots(),
        "ident": np.eye(P, dtype=np.float32),
        "tri": np.tile(np.tril(np.ones((EXPERTS, EXPERTS), np.float32), -1).reshape(-1), TILES),
        "wr_t": a["router_weight"].T,
        "rb": a["router_bias"],
        "gu_t": a["gate_up_proj"].reshape(-1, d).T,
        "gu_bias": a["gate_up_proj_bias"].reshape(-1, P).T,
        "dn_t": a["down_proj"].reshape(EXPERTS, d, 2, P).transpose(3, 0, 2, 1).reshape(P, CHUNKS, d),
        "dn_bias": a["down_proj_bias"],
    }
    arrays = {k: np.ascontiguousarray(v) for k, v in arrays.items()}

    nc = bacc.Bacc("TRN2", target_bir_lowering=False, num_devices=1)
    ins = {k: nc.dram_tensor(f"in_{k}", v.shape, mybir.dt.from_np(v.dtype), kind="ExternalInput").ap()
           for k, v in arrays.items()}
    out = nc.dram_tensor("out_y", (batch * seq, d), F32, kind="ExternalOutput").ap()
    build_layer(nc, ins, out)
    r = run_bass_kernel_spmd(nc, [{f"in_{k}": v for k, v in arrays.items()}], core_ids=[0])
    return r.results[0]["out_y"].reshape(batch, seq, d)
```

```python
from contextlib import ExitStack
import math

import numpy as np

import concourse.bass as bass
from concourse import mybir

F32 = mybir.dt.float32
F32R = mybir.dt.float32r
ACT = mybir.ActivationFunctionType
ALU = mybir.AluOpType
AX = mybir.AxisListType

P = 128
HEADS, HD = 16, 8
NG = 4
BUCKETS, MAX_DISTANCE = 32, 128
SCALE = HD ** -0.5
EPS = 1e-5
EXPERTS, TOP_K, INTER = 8, 4, 256
ALPHA, LIMIT = 1.702, 7.0
CLIP = ALPHA * LIMIT / (1.0 + math.exp(-ALPHA * LIMIT))
MASKED = -1.0e30
SPAN = 384
SEQ = 256
T = 512
TILES = T // P
CHUNKS = EXPERTS * INTER // P
AHEAD = 6
LAG = 9
MAX_BESIDE = (2, 2, 2, 3, 3, 4, 4, 4, 4, 4)
SU_SLOTS, AW_SLOTS, P_SLOTS = 4, 9, 12


class Count:

    def __init__(self, per, by=1):
        self.per, self.by, self.base, self.local, self.t = per, by, 0, 0, None

    def begin(self, t):
        if self.t is None:
            self.base = self.local
        else:
            assert self.local in (0, self.per), (self.local, self.per)
        self.t, self.local = t, 0

    def step(self, n=1):
        self.local += n
        return self.now()

    def now(self):
        if self.t is None:
            return self.local * self.by
        return self.t * (self.per * self.by) + (self.base + self.local) * self.by


def build_layer(nc, ins, out):
    ctx = ExitStack()
    with ctx:
        def sb(name, shape, dt=F32):
            return ctx.enter_context(nc.sbuf_tensor(name, shape, dt))

        def bank(name):
            return ctx.enter_context(nc.psum_tensor(name, [P, 512], F32))

        def sem(name):
            return ctx.enter_context(nc.semaphore(name))

        ident = sb("ident", [P, P])
        wqk_hi = sb("wqk_hi", [P, 2, P], F32R)
        wqk_lo = sb("wqk_lo", [P, 2, P], F32R)
        wv = sb("wv", [P, P])
        wo_t = sb("wo_t", [P, P])
        wr_t = sb("wr_t", [P, EXPERTS])
        gu_hi = sb("gu_hi", [P, 4096], F32R)
        gu_lo = sb("gu_lo", [P, 4096], F32R)
        dn_t = sb("dn_t", [P, CHUNKS, P])
        dn_bias = sb("dn_bias", [EXPERTS, P])
        gu_bias = sb("gu_bias", [P, 32])
        gate_bias = sb("gate_bias", [P, 32])
        up_bias = sb("up_bias", [P, 32])
        cols = sb("cols", [P, 3])
        bv_rows = sb("bv_rows", [P, P])
        rb_rows = sb("rb_rows", [P, EXPERTS])
        tri = sb("tri", [P, TILES * 64])
        rel = sb("rel", [BUCKETS, HEADS])
        bias = sb("bias", [P, HEADS, 384])
        minus_half = sb("minus_half", [P, TILES])
        x_in = sb("x_in", [P, TILES, P])
        x_res = sb("x_res", [P, TILES, P])
        stats = sb("stats", [P, TILES, 6])
        mean_var = sb("mean_var", [P, TILES, 2])
        var_eps = sb("var_eps", [P, TILES])
        rstd = sb("rstd", [P, TILES])
        xn = sb("xn", [P, TILES, P])
        attn_t = sb("attn_t", [P, T])
        xn_t = sb("xn_t", [P, T])
        y_t = xn_t
        xn_rev = sb("xn_rev", [P, T])
        xn_hi = sb("xn_hi", [P, T], F32R)
        xn_lo = sb("xn_lo", [P, T], F32R)
        qk = sb("qk", [P, 2, T])
        qk_hi = sb("qk_hi", [P, 2, T], F32R)
        qk_lo = sb("qk_lo", [P, 2, T], F32R)
        q_rows = sb("q_rows", [P, NG, T], F32R)
        k_rows = sb("k_rows", [P, NG, T], F32R)
        v_one = sb("v_one", [P, TILES, HEADS * (HD + 1) + 32])
        v_heads = v_one[:, :, 0:HEADS * (HD + 1)].rearrange("p q (h w) -> p q h w", h=HEADS)
        row_max = sb("row_max", [P, TILES, HEADS])
        neg_max = sb("neg_max", [HEADS, T])
        probs = sb("probs", [P, P_SLOTS, 384])
        heads_t = sb("heads_t", [P, NG, T])
        recip = sb("recip", [P, TILES, HEADS])
        attn = sb("attn", [P, TILES, P])
        logits = sb("logits", [P, TILES, EXPERTS])
        shifted = sb("shifted", [P, TILES, EXPERTS])
        exps = sb("exps", [P, TILES * EXPERTS])
        top = sb("top", [P, TILES])
        diff = sb("diff", [P, TILES * 64])
        ahead = sb("ahead", [P, TILES * 64])
        rank = sb("rank", [P, TILES * EXPERTS])
        kept = sb("kept", [P, TILES * EXPERTS])
        total = sb("total", [P, TILES])
        total_inv = sb("total_inv", [P, TILES])
        combine = sb("combine", [P, TILES, EXPERTS])
        comb_t = sb("comb_t", [EXPERTS, T])
        comb_scaled = neg_max[0:EXPERTS, :]
        comb_all = sb("comb_all", [P, EXPERTS, T])
        s_buf = sb("s_buf", [P, SU_SLOTS, T])
        u_buf = sb("u_buf", [P, SU_SLOTS, T])
        aw_buf = sb("aw_buf", [P, AW_SLOTS, T])
        gu_raw = probs[:, :, :].rearrange("p s c -> p (s c)")
        wqk = aw_buf[:, 0, 0:2 * P].rearrange("p (w c) -> p w c", w=2)
        onehot = aw_buf[0:BUCKETS, 1, 0:SPAN]
        dist = aw_buf[0:HEADS, 3, 0:SPAN]
        dist_dram = nc.dram_tensor("dist_dram", [HEADS, SPAN], F32, kind="Internal")

        class Bank:

            def __init__(self, name, per, start=0):
                self.ps, self.full, self.free = bank(name), sem(name + "_full"), sem(name + "_free")
                self.per, self.start = per, start

        GATE = Bank("gate", 1 + CHUNKS)
        UP = Bank("up", 1 + CHUNKS)
        S = [Bank("scores0", 32), Bank("scores1", 32, start=1)]
        PV = Bank("pv", 8, start=1)
        Y = Bank("y", 1, start=1)
        M0 = Bank("misc0", 7)
        M1 = Bank("misc1", 6)
        BANKS = [GATE, UP, *S, PV, Y, M0, M1]

        loaded = {n: sem(n + "_loaded") for n in ("attn_w", "first", "small", "gu_half0", "gu_half1", "dn", "hot", "bias",
                                                  "bias_rest", "bias_again", "x", "x_res")}
        dist_ready, dist_stored = sem("dist_ready"), sem("dist_stored")
        filled = sem("filled")
        attn_w_hi, attn_w_split = sem("attn_w_hi"), sem("attn_w_split")
        gu_hi_done, gu_split = sem("gu_hi_done"), sem("gu_split")
        biases_ready = sem("biases_ready")
        var_ready, rstd_ready, xn_ready = sem("var_ready"), sem("rstd_ready"), sem("xn_ready")
        xn_split, xn_rev_ready, qk_split = sem("xn_split"), sem("xn_rev_ready"), sem("qk_split")
        rows_loaded, max_loaded = sem("rows_loaded"), [sem("max0_loaded"), sem("max1_loaded")]
        shifted_ready, exps_ready, combine_ready = sem("shifted_ready"), sem("exps_ready"), sem("combine_ready")
        comb_row_loaded, comb_all_ready = sem("comb_row_loaded"), sem("comb_all_ready")
        probs_ready = sem("probs_ready")
        act_ready, weighted = sem("act_ready"), sem("weighted")
        slot_free = sem("slot_free")
        stored = sem("stored")
        dve_step, pool_step = sem("dve_step"), sem("pool_step")
        x_view = ins["x"].rearrange("(n q p) c -> n p q c", p=P, q=TILES)
        out_view = out.rearrange("(n q p) c -> n p q c", p=P, q=TILES)
        N = x_view.shape[0]

        def units(first, last):
            return [(u, u // 16, u % 4, u % 16 // 4) for u in range(first, last)]

        def beside(k):
            first = sum(MAX_BESIDE[:k - AHEAD])
            return units(first, first + MAX_BESIDE[k - AHEAD])

        class Program:

            def __init__(self, eng):
                self.eng = eng
                self.uses = {id(b): Count(b.per) for b in BANKS}
                self.counts = {}
                self.value = None

            def count(self, s, per, by=1):
                return self.counts.setdefault(id(s), Count(per, by))

            def begin(self, t):
                for c in [*self.uses.values(), *self.counts.values()]:
                    c.begin(t)

            def wait(self, s, n):
                if not isinstance(n, int):
                    self.value = self.value or self.eng.alloc_register("awaited")
                    self.eng.reg_add(self.value, n, 0)
                    self.eng.wait_ge(dist_ready, 1)
                    n = self.value
                self.eng.wait_ge(s, n)

            def fill(self, b):
                n = self.uses[id(b)].step() - 1 + b.start
                if not isinstance(n, int) or n > 0:
                    self.eng.wait_ge(b.free, n)

            def released(self, b):
                return self.uses[id(b)].now() + b.start

            def read(self, b, apart=False):
                n = self.uses[id(b)].step()
                (self.wait if apart else self.eng.wait_ge)(b.full, n)

            def skip(self, b, n=1):
                return self.uses[id(b)].step(n)

        block = ctx.enter_context(nc.Block())

        @block.sync
        def _(sp):
            pr = Program(sp)
            xn_ready_n = pr.count(xn_ready, 1)
            stored_n = pr.count(stored, 1, 16)
            weighted_n, qk_split_n = pr.count(weighted, CHUNKS), pr.count(qk_split, 1, 2)
            first = [(ident[:], ins["ident"]), (cols[:], ins["cols"]), (wr_t[:], ins["wr_t"])]
            small = [(rb_rows[:], ins["rb"].partition_broadcast(P)), (tri[:], ins["tri"].partition_broadcast(P)),
                     (gu_bias[:], ins["gu_bias"]), (wv[:], ins["wv"]), (bv_rows[:], ins["bv"].partition_broadcast(P)),
                     (dn_bias[:], ins["dn_bias"]), (wo_t[:], ins["wo_t"])]
            sp.dma_start(x_in[:], x_view[0]).then_inc(loaded["x"], 16)
            sp.dma_start(rel[:], ins["rel"]).then_inc(loaded["hot"], 16)
            sp.dma_start(onehot, ins["onehot"]).then_inc(loaded["hot"], 16)
            sp.dma_start(wqk, ins["wqk"]).then_inc(loaded["attn_w"], 16)
            for dst, src in first:
                sp.dma_start(dst, src).then_inc(loaded["first"], 16)
            for half in range(2):
                for c in range(4 * half, 4 * half + 4):
                    sp.dma_start(gu_raw[:, 512 * c:512 * c + 512],
                                 ins["gu_t"][:, 512 * c:512 * c + 512]).then_inc(loaded[f"gu_half{half}"], 16)
                if half == 0:
                    for dst, src in small:
                        sp.dma_start(dst, src).then_inc(loaded["small"], 16)
            sp.wait_ge(dist_ready, 1)
            sp.dma_start(dist_dram.ap(), dist).then_inc(dist_stored, 16)
            sp.wait_ge(xn_ready, xn_ready_n.step())
            sp.dma_start(x_in[:], x_view[1]).then_inc(loaded["x"], 16)
            sp.wait_ge(dist_stored, 16)
            def load_bias(g, c0, c1, semaphore):
                sp.dma_start(bias[:, g::NG, c0:c1],
                             bass.AP(dist_dram, g * SPAN, [[1, P], [NG * SPAN, HEADS // NG], [1, c1 - c0]])).then_inc(semaphore, 16)

            load_bias(0, 0, 256, loaded["bias"])
            load_bias(1, 0, 256, loaded["bias_rest"])

            def load_comb_row():
                pr.wait(M1.free, pr.skip(M1))
                if pr.uses[id(M1)].t is not None:
                    pr.wait(weighted, weighted_n.now())
                sp.dma_start(comb_all[0:1, :, :], comb_scaled).then_inc(comb_row_loaded, 16)

            def load_rows():
                pr.wait(qk_split, qk_split_n.step())
                for rows, which, parts in ((q_rows, 0, (qk_hi, qk_hi, qk_lo)), (k_rows, 1, (qk_hi, qk_lo, qk_hi))):
                    for a, part in enumerate(parts):
                        sp.dma_start(rows[a:P:4].bitcast(F32), part[:, which, :].bitcast(F32)).then_inc(rows_loaded, 16)

            sp.wait_ge(filled, 4)
            load_comb_row()
            load_rows()
            for g in range(2, NG):
                load_bias(g, 0, 256, loaded["bias_rest"])
            for g in range(NG):
                load_bias(g, 256, 384, loaded["bias_again"])
            sp.dma_start(x_res[:], x_view[0]).then_inc(loaded["x_res"], 16)
            sp.dma_start(dn_t[:], ins["dn_t"]).then_inc(loaded["dn"], 16)
            pr.skip(M1)

            def body(t, last):
                pr.begin(t)
                if not last:
                    pr.wait(xn_ready, xn_ready_n.step())
                    sp.dma_start(x_in[:], x_view[(t + 2) % N]).then_inc(loaded["x"], 16)
                for b in range(2):
                    pr.wait(M1.free, pr.skip(M1))
                    sp.dma_start(q_rows[31:P:32, :, b * SEQ:b * SEQ + SEQ].bitcast(F32),
                                 neg_max[:, b * SEQ:b * SEQ + SEQ]).then_inc(max_loaded[b], 16)
                weighted_n.step(CHUNKS - AHEAD + 1)
                if not last:
                    load_comb_row()
                    weighted_n.step(AHEAD - 1)
                    for b in range(2):
                        pr.wait(S[b].full, pr.skip(S[b], 32))
                    load_rows()
                    pr.skip(M1)
                pr.skip(M1, 2)
                pr.wait(M0.free, pr.skip(M0, 7 if not last else 5))
                sp.dma_start(out_view[t], x_res[:]).then_inc(stored, 16)
                stored_n.step()
                pr.wait(stored, stored_n.now())
                if not last:
                    sp.dma_start(x_res[:], x_view[t + 1]).then_inc(loaded["x_res"], 16)

            pr.skip(M0, 2)
            weighted_n.step(AHEAD - 1)
            pr.skip(S[0])
            with sp.Fori(0, N - 1) as t:
                body(t, False)
            body(N - 1, True)

        @block.tensor
        def _(pe):
            pr = Program(pe)
            xn_ready_n, xn_split_n = pr.count(xn_ready, 1), pr.count(xn_split, 1)
            rows_n, max_n = pr.count(rows_loaded, 6, 16), [pr.count(m, 1, 16) for m in max_loaded]
            comb_n, weighted_n = pr.count(combine_ready, 1), pr.count(weighted, CHUNKS)
            probs_n, rev_n = pr.count(probs_ready, 16), pr.count(xn_rev_ready, 1)
            freed = {}

            def split_product(dst, hi, lo, rhs_hi, rhs_lo):
                nc.tensor.matmul(dst, lo, rhs_hi, start=True, stop=False)
                nc.tensor.matmul(dst, hi, rhs_lo, start=False, stop=False)
                return nc.tensor.matmul(dst, hi, rhs_hi, start=False, stop=True)

            def transpose_x():
                pr.fill(M0)
                pe.wait_ge(xn_ready, xn_ready_n.step())
                for q in range(TILES):
                    mm = nc.tensor.transpose(M0.ps[:, q * P:q * P + P], xn[:, q, :], ident[:])
                mm.then_inc(M0.full, 1)
                freed["xn_t"] = pr.released(M0)

            def router():
                pe.wait_ge(M0.free, freed["xn_t"])
                pr.fill(M0)
                for q in range(TILES):
                    mm = nc.tensor.matmul(M0.ps[:, q * EXPERTS:(q + 1) * EXPERTS], xn_t[:, q * P:q * P + P], wr_t[:],
                                          start=True, stop=True)
                mm.then_inc(M0.full, 1)

            def project_q():
                pe.wait_ge(xn_split, xn_split_n.step())
                pr.fill(GATE)
                split_product(GATE.ps[:], wqk_hi[:, 0, :], wqk_lo[:, 0, :], xn_hi[:], xn_lo[:]).then_inc(GATE.full, 1)

            def project_k():
                pr.fill(UP)
                split_product(UP.ps[:], wqk_hi[:, 1, :], wqk_lo[:, 1, :], xn_hi[:, ::-1], xn_lo[:, ::-1]).then_inc(UP.full, 1)

            def project_v():
                pr.fill(M1)
                pe.wait_ge(xn_rev_ready, rev_n.step())
                for q in range(TILES):
                    mm = nc.tensor.matmul(M1.ps[:, q * P:q * P + P], xn_rev[:, q * P:q * P + P], wv[:], start=True, stop=True)
                mm.then_inc(M1.full, 1)

            def transpose_combine():
                pr.fill(M1)
                pe.wait_ge(combine_ready, comb_n.step())
                for q in range(TILES):
                    mm = nc.tensor.transpose(M1.ps[0:EXPERTS, q * P:q * P + P], combine[:, q, :], ident[:])
                mm.then_inc(M1.full, 1)

            def gate_up_half(k, half):
                b, (e, c) = (GATE, UP)[half], divmod(k, 2)
                w = slice(e * 512 + half * 256 + c * P, e * 512 + half * 256 + c * P + P)
                pr.fill(b)
                split_product(b.ps[:], gu_hi[:, w], gu_lo[:, w], xn_hi[:], xn_lo[:]).then_inc(b.full, 1)

            def gate_up(k):
                gate_up_half(k, 0)
                gate_up_half(k, 1)

            def down(k):
                if k == 0:
                    pr.fill(Y)
                    nc.tensor.matmul(Y.ps[:], dn_bias[:], comb_t[:], start=True, stop=False)
                pe.wait_ge(weighted, weighted_n.step())
                nc.tensor.matmul(Y.ps[:], dn_t[:, k, :], aw_buf[:, k % AW_SLOTS, :], start=False, stop=False).then_inc(slot_free, 1)

            def max_scores(u, b, r, g):
                s = S[u % 2]
                pr.fill(s)
                rows = slice(32 * r, 32 * r + 31)
                q, k = q_rows[rows, g, b * SEQ:(b + 1) * SEQ], k_rows[rows, g, (1 - b) * SEQ:(2 - b) * SEQ]
                nc.tensor.matmul(s.ps[:, 0:P], q[:, 0:P], k[:, P:SEQ], start=True, stop=True)
                mm = nc.tensor.matmul(s.ps[:, P:P + SEQ], q[:, P:SEQ], k, start=True, stop=True)
                mm.then_inc(s.full, 1)
                freed["max", b, u % 2] = pr.released(s)

            def transpose_max(b):
                for s in S:
                    pe.wait_ge(s.free, freed["max", b, s is S[1]])
                pr.fill(M1)
                for q in range(2):
                    mm = nc.tensor.transpose(M1.ps[0:HEADS, q * P:q * P + P], row_max[:, 2 * b + q, :], ident[:])
                mm.then_inc(M1.full, 1)

            def prob_scores(u, b, r, g):
                s = S[u % 2]
                pr.fill(s)
                rows = slice(32 * r, 32 * r + 32)
                q, k = q_rows[rows, g, b * SEQ:(b + 1) * SEQ], k_rows[rows, g, (1 - b) * SEQ:(2 - b) * SEQ]
                nc.tensor.matmul(s.ps[:, 0:SEQ], k[:, P:SEQ], q, start=True, stop=True)
                nc.tensor.matmul(s.ps[:, SEQ:SEQ + P], k[:, 0:P], q[:, P:SEQ], start=True, stop=True).then_inc(s.full, 1)

            def weigh_values(grp, kt):
                b, g = divmod(grp, 4)
                if kt == 0:
                    pr.fill(PV)
                    pe.wait_ge(probs_ready, probs_n.step(2))
                for r in range(4):
                    h, p = 4 * r + g, probs[:, (4 * grp + r) % P_SLOTS, :]
                    mm = nc.tensor.matmul(PV.ps[32 * r:32 * r + 32, kt * P:256],
                                          v_one[:, 2 * (1 - b) + 1 - kt, h * (HD + 1):h * (HD + 1) + 32],
                                          p[:, 256 * kt:256 + 128 * kt],
                                          start=(kt == 0), stop=(kt == 1), tile_position=(0, 32 * r))
                if kt == 1:
                    mm.then_inc(PV.full, 1)
                    freed["heads", grp] = pr.released(PV)

            def transpose_heads(q):
                pr.fill(M0)
                pe.wait_ge(PV.free, freed["heads", 4 * (q // 2) + 3])
                for g in range(NG):
                    mm = nc.tensor.transpose(M0.ps[:, g * P:g * P + P], heads_t[:, g, q * P:q * P + P], ident[:])
                mm.then_inc(M0.full, 1)
                freed["norm", q] = pr.released(M0)

            def transpose_attn(b):
                pe.wait_ge(M0.free, freed["norm", 2 * b + 1])
                pr.fill(M1)
                for q in range(2):
                    mm = nc.tensor.transpose(M1.ps[:, q * P:q * P + P], attn[:, 2 * b + q, :], ident[:])
                mm.then_inc(M1.full, 1)
                freed["attn_t", b] = pr.released(M1)

            def project_out():
                pe.wait_ge(M1.free, freed["attn_t", 1])
                nc.tensor.matmul(Y.ps[:], wo_t[:], attn_t[:], start=False, stop=True).then_inc(Y.full, 1)

            def transpose_y():
                pr.fill(M0)
                pe.wait_ge(Y.free, pr.released(Y))
                for q in range(TILES):
                    mm = nc.tensor.transpose(M0.ps[:, q * P:q * P + P], y_t[:, q * P:q * P + P], ident[:])
                mm.then_inc(M0.full, 1)

            pe.wait_ge(loaded["hot"], 32)
            pr.fill(S[0])
            nc.tensor.matmul(S[0].ps[0:HEADS, 0:SPAN], rel[:], onehot, start=True, stop=True).then_inc(S[0].full, 1)
            for i, (semaphore, n) in enumerate(((S[1].free, 1), (Y.free, 1), (slot_free, AW_SLOTS), (PV.free, 1))):
                nc.tensor.matmul(PV.ps[0:HEADS, 4 * i:4 * i + 4], rel[:], onehot[:, 0:4], start=True, stop=True).then_inc(semaphore, n)
            pe.wait_ge(loaded["first"], 16 * 3)
            transpose_x()
            pe.wait_ge(attn_w_split, 1)
            router()
            project_q()
            project_k()
            pe.wait_ge(gu_split, 1)
            gate_up(0)
            transpose_combine()
            pe.wait_ge(loaded["small"], 16 * 7)
            project_v()
            for k in range(1, AHEAD):
                if k % 2 == 0:
                    pe.wait_ge(gu_split, k // 2 + 1)
                gate_up(k)

            def body(t, last):
                pr.begin(t)
                pe.wait_ge(rows_loaded, rows_n.step(6))
                for k in range(AHEAD, CHUNKS):
                    if k % 2 == 0:
                        pe.wait_ge(gu_split, k // 2 + 1)
                    heads = beside(k)
                    for u in heads[:1]:
                        max_scores(*u)
                    gate_up_half(k, 0)
                    for u in heads[1:2]:
                        max_scores(*u)
                    gate_up_half(k, 1)
                    for u in heads[2:3]:
                        max_scores(*u)
                    if k == 12:
                        transpose_max(0)
                    if k == LAG:
                        pe.wait_ge(loaded["dn"], 16)
                    if k >= LAG:
                        down(k - LAG)
                    for u in heads[3:]:
                        max_scores(*u)
                if not last:
                    transpose_x()
                late = iter(range(CHUNKS - LAG, CHUNKS))
                down(next(late))
                transpose_max(1)
                for grp in range(8):
                    if grp % 4 == 0:
                        pe.wait_ge(max_loaded[grp // 4], max_n[grp // 4].step())
                    first, second = units(4 * grp, 4 * grp + 2), units(4 * grp + 2, 4 * grp + 4)
                    for u in first:
                        prob_scores(*u)
                    if grp >= 2:
                        weigh_values(grp - 2, 1)
                    if grp in (0, 1, 3, 4):
                        down(next(late))
                    if not last:
                        if grp == 2:
                            project_q()
                        if grp == 5:
                            transpose_combine()
                        if grp == 7:
                            gate_up_half(0, 1)
                    for u in second:
                        prob_scores(*u)
                    if grp >= 1:
                        weigh_values(grp - 1, 0)
                    if grp == 0:
                        down(next(late))
                    if grp == 5:
                        transpose_heads(0)
                    if grp == 6:
                        transpose_heads(1)
                    if not last:
                        if grp == 1:
                            router()
                        if grp == 2:
                            project_k()
                        if grp == 4:
                            gate_up_half(0, 0)
                weigh_values(6, 1)
                if not last:
                    project_v()
                down(next(late))
                weigh_values(7, 0)
                weigh_values(7, 1)
                down(next(late))
                transpose_heads(2)
                down(next(late))
                transpose_attn(0)
                transpose_heads(3)
                if not last:
                    gate_up(1)
                    gate_up_half(2, 0)
                transpose_attn(1)
                if not last:
                    gate_up_half(2, 1)
                    gate_up(3)
                for k in late:
                    down(k)
                project_out()
                if not last:
                    gate_up(4)
                transpose_y()
                if not last:
                    gate_up(5)

            with pe.Fori(0, N - 1) as t:
                body(t, False)
            body(N - 1, True)

        @block.scalar
        def _(act):
            pr = Program(act)
            shifted_n = pr.count(shifted_ready, 1)
            act_n, weighted_n = pr.count(act_ready, CHUNKS), pr.count(weighted, CHUNKS)

            def copy_x():
                pr.read(M0)
                nc.scalar.copy(xn_t[:], M0.ps[:])
                nc.scalar.copy(xn_hi[:], M0.ps[:]).then_inc(M0.free, 1)
                pr.skip(M0)

            def copy_qk():
                for w, b in enumerate((GATE, UP)):
                    pr.read(b)
                    nc.scalar.activation(qk[:, w, :], b.ps[:], ACT.Identity, bias=cols[:, w:w + 1])
                    nc.scalar.activation(qk_hi[:, w, :], b.ps[:], ACT.Identity, bias=cols[:, w:w + 1]).then_inc(b.free, 1)

            def router_exp():
                act.wait_ge(shifted_ready, shifted_n.step())
                nc.scalar.activation(exps[:], shifted[:].rearrange("p q e -> p (q e)"), ACT.Exp).then_inc(exps_ready, 1)

            def copy_combine():
                pr.read(M1)
                nc.scalar.mul(comb_scaled, M1.ps[0:EXPERTS, :], 1.0 / ALPHA)
                nc.scalar.copy(comb_t[:], M1.ps[0:EXPERTS, :]).then_inc(M1.free, 1)

            def gate_half(k):
                n = act_n.step() - SU_SLOTS
                weighted_n.step()
                if not isinstance(n, int) or n > 0:
                    act.wait_ge(act_ready, n)
                    act.wait_ge(weighted, n)
                pr.read(GATE)
                col = 4 * (k // 2) + k % 2
                nc.scalar.activation(s_buf[:, k % SU_SLOTS, :], GATE.ps[:], ACT.Silu, bias=gate_bias[:, col:col + 1],
                                     scale=ALPHA).then_inc(GATE.free, 1)

            def up_half(k):
                col = 4 * (k // 2) + k % 2
                pr.read(UP)
                nc.scalar.activation(u_buf[:, k % SU_SLOTS, :], UP.ps[:], ACT.Identity,
                                     bias=up_bias[:, col + 2:col + 3]).then_inc(UP.free, 1)

            def gate_up(k):
                gate_half(k)
                up_half(k)

            def negate_max(b):
                pr.read(M1)
                nc.scalar.activation(neg_max[:, b * SEQ:b * SEQ + SEQ], M1.ps[0:HEADS, 0:SEQ], ACT.Copy,
                                     scale=-1.0).then_inc(M1.free, 1)

            def exponents(u):
                for s in S:
                    pr.skip(s)
                    act.wait_ge(s.free, pr.released(s))
                p = probs[:, u % P_SLOTS:u % P_SLOTS + 2, :]
                nc.scalar.activation(p, p, ACT.Exp).then_inc(probs_ready, 1)

            def copy_heads(grp):
                b, g = divmod(grp, 4)
                pr.read(PV)
                nc.scalar.copy(heads_t[:, g, b * SEQ:b * SEQ + SEQ], PV.ps[:, 0:SEQ]).then_inc(PV.free, 1)

            def copy_attn(b):
                pr.read(M1)
                nc.scalar.copy(attn_t[:, b * SEQ:b * SEQ + SEQ], M1.ps[:, 0:SEQ]).then_inc(M1.free, 1)

            def copy_y():
                pr.read(Y)
                nc.scalar.activation(y_t[:], Y.ps[:], ACT.Identity, bias=cols[:, 2:3]).then_inc(Y.free, 1)

            pr.read(S[0])
            nc.scalar.mul(dist, S[0].ps[0:HEADS, 0:SPAN], SCALE).then_inc(S[0].free, 1)
            act.wait_ge(loaded["attn_w"], 16)
            nc.scalar.copy(wqk_hi[:], wqk).then_inc(attn_w_hi, 1)
            act.wait_ge(loaded["first"], 16 * 3)
            copy_x()

            def round_gu(c):
                if c % 4 == 0:
                    act.wait_ge(loaded[f"gu_half{c // 4}"], 16 * 4)
                nc.scalar.copy(gu_hi[:, 512 * c:512 * c + 512], gu_raw[:, 512 * c:512 * c + 512]).then_inc(gu_hi_done, 1)

            round_gu(0)
            round_gu(1)
            copy_qk()
            router_exp()
            for c in range(2, 4):
                round_gu(c)
            copy_combine()
            pr.skip(M1)
            act.wait_ge(loaded["small"], 16 * 7)
            nc.scalar.mul(gate_bias[:], gu_bias[:], ALPHA)
            nc.scalar.add(up_bias[:], gu_bias[:], 1.0).then_inc(biases_ready, 1)
            act.wait_ge(biases_ready, 1)
            gate_up(0)
            gate_up(1)
            for c in range(4, 8):
                round_gu(c)
            for k in range(2, AHEAD):
                gate_up(k)

            def body(t, last):
                pr.begin(t)
                for k in range(AHEAD, CHUNKS):
                    gate_up(k)
                    if k == 13:
                        negate_max(0)
                if not last:
                    copy_x()
                negate_max(1)
                for s in S:
                    pr.skip(s, 16)
                for grp in range(8):
                    for u in (4 * grp, 4 * grp + 2):
                        exponents(u)
                    if grp:
                        copy_heads(grp - 1)
                    if grp == 2 and not last:
                        copy_qk()
                    if grp == 3 and not last:
                        router_exp()
                    if grp == 5 and not last:
                        copy_combine()
                copy_heads(7)
                if not last:
                    pr.skip(M1)
                    gate_up(0)
                copy_attn(0)
                if not last:
                    gate_up(1)
                    gate_half(2)
                copy_attn(1)
                if not last:
                    up_half(2)
                    gate_up(3)
                copy_y()
                pr.skip(M0, 5)
                if not last:
                    gate_up(4)
                    gate_up(5)

            with act.Fori(0, N - 1) as t:
                body(t, False)
            body(N - 1, True)

        @block.vector
        def _(dve):
            pr = Program(dve)
            x_n, xres_n = pr.count(loaded["x"], 1, 16), pr.count(loaded["x_res"], 1, 16)
            rstd_n, exps_n = pr.count(rstd_ready, 1), pr.count(exps_ready, 1)
            own = pr.count(dve_step, CHUNKS + 2 + 8 + TILES)
            pv_n = pr.count(PV.full, 8)
            done = {}

            def gives(name, ins):
                ins.then_inc(dve_step, 1)
                done[name] = own.step()

            def needs(name):
                dve.wait_ge(dve_step, done[name])

            def row_stats():
                dve.wait_ge(loaded["x"], x_n.step())
                for q in range(TILES):
                    i = nc.vector.bn_stats(stats[:, q, :], x_in[:, q, :])
                gives("stats", i)

            def mean_variance():
                pr.wait(dve_step, done["stats"])
                for q in range(TILES):
                    i = nc.vector.bn_aggr(mean_var[:, q, :], stats[:, q, :])
                gives("mean_var", i)

            def add_eps():
                needs("mean_var")
                nc.vector.tensor_scalar(var_eps[:], mean_var[:, :, 1], EPS, None, ALU.add).then_inc(var_ready, 1)

            def normalise():
                dve.wait_ge(rstd_ready, rstd_n.step())
                for q in range(TILES):
                    i = nc.vector.tensor_scalar(xn[:, q, :], x_in[:, q, :], mean_var[:, q, 0:1], rstd[:, q:q + 1],
                                                ALU.subtract, ALU.mult)
                i.then_inc(xn_ready, 1)

            def add_router_bias():
                pr.read(M0)
                nc.vector.tensor_tensor(logits[:], M0.ps[:, 0:32].rearrange("p (q e) -> p q e", q=TILES),
                                        rb_rows[:].unsqueeze(1).broadcast_to([P, TILES, EXPERTS]), ALU.add).then_inc(M0.free, 1)
                done["logits"] = pr.released(M0)

            def largest_logit():
                dve.wait_ge(M0.free, done["logits"])
                gives("top", nc.vector.tensor_reduce(top[:], logits[:], AX.X, ALU.max))

            def compare_logits():
                four = [P, TILES, EXPERTS, EXPERTS]
                gives("diff", nc.vector.tensor_tensor(diff[:].rearrange("p (q i j) -> p q i j", q=TILES, i=EXPERTS),
                                                      logits[:].unsqueeze(2).broadcast_to(four),
                                                      logits[:].unsqueeze(3).broadcast_to(four), ALU.subtract))

            def shift_logits():
                needs("top")
                nc.vector.tensor_tensor(shifted[:], logits[:], top[:].unsqueeze(2).broadcast_to([P, TILES, EXPERTS]),
                                        ALU.subtract).then_inc(shifted_ready, 1)

            def equal_or_greater():
                needs("diff")
                gives("ties", nc.vector.scalar_tensor_tensor(ahead[:], diff[:], 0.0, tri[:], ALU.is_ge, ALU.mult))

            def greater():
                needs("ties")
                gives("ahead", nc.vector.scalar_tensor_tensor(ahead[:], diff[:], 0.0, ahead[:], ALU.is_gt, ALU.max))

            def count_ahead():
                needs("ahead")
                gives("rank", nc.vector.tensor_reduce(rank[:], ahead[:].rearrange("p (i j) -> p i j", j=EXPERTS), AX.X, ALU.add))

            def keep_top():
                needs("rank")
                dve.wait_ge(exps_ready, exps_n.step())
                gives("kept", nc.vector.scalar_tensor_tensor(kept[:], rank[:], float(TOP_K), exps[:], ALU.is_lt, ALU.mult))

            def sum_kept():
                needs("kept")
                gives("total", nc.vector.tensor_reduce(total[:], kept[:].rearrange("p (q e) -> p q e", q=TILES), AX.X, ALU.add))

            def invert_total():
                needs("total")
                gives("total_inv", nc.vector.reciprocal(total_inv[:], total[:]))

            def combine_weights():
                needs("total_inv")
                nc.vector.tensor_tensor(combine[:], kept[:].rearrange("p (q e) -> p q e", q=TILES),
                                        total_inv[:].unsqueeze(2).broadcast_to([P, TILES, EXPERTS]),
                                        ALU.mult).then_inc(combine_ready, 1)

            def copy_v():
                pr.read(M1)
                nc.vector.tensor_tensor(v_heads[:, :, :, 0:HD], M1.ps[:].rearrange("p (q h d) -> p q h d", q=TILES, h=HEADS),
                                        bv_rows[:].rearrange("p (h d) -> p h d", h=HEADS).unsqueeze(1).broadcast_to([P, TILES, HEADS, HD]),
                                        ALU.add).then_inc(M1.free, 1)

            def clip_up(k):
                dve.wait_ge(GATE.free, pr.skip(GATE))
                dve.wait_ge(UP.free, pr.skip(UP))
                u = u_buf[:, k % SU_SLOTS, :]
                gives("clipped", nc.vector.tensor_scalar(u, u, LIMIT + 1.0, 1.0 - LIMIT, ALU.min, ALU.max))

            def activate(k):
                s, u = s_buf[:, k % SU_SLOTS, :], u_buf[:, k % SU_SLOTS, :]
                needs("clipped")
                nc.vector.scalar_tensor_tensor(s, s, CLIP, u, ALU.min, ALU.mult).then_inc(act_ready, 1)

            def reduce_max(u, b, r, g):
                s, h = S[u % 2], 4 * r + g
                pr.read(s, apart=True)
                for qt, c0, c1 in ((0, 0, 128), (1, 128, 384)):
                    i = nc.vector.tensor_tensor_reduce(s.ps[:, c0:c1], s.ps[:, c0:c1], bias[:, h, 0:c1 - c0], 1.0, -3.0e38,
                                                       ALU.add, ALU.max, row_max[:, 2 * b + qt, h:h + 1])
                i.then_inc(s.free, 1)

            def add_bias(u, b, r, g):
                s, h = S[u % 2], 4 * r + g
                if u >= P_SLOTS and u % 4 == 0:
                    dve.wait_ge(PV.full, pv_n.step())
                pr.read(s)
                nc.vector.tensor_tensor(probs[:, u % P_SLOTS, :], s.ps[:, 0:384], bias[:, h, :], ALU.add).then_inc(s.free, 1)

            def norm_heads(q):
                pr.read(M0)
                v = M0.ps[:].rearrange("p (g r w) -> p r g w", g=NG, r=4)
                gives("recip", nc.vector.reciprocal(recip[:, q, :].rearrange("p (r g) -> p r g", g=NG), v[:, :, :, HD]))
                needs("recip")
                nc.vector.tensor_tensor(attn[:, q, :].rearrange("p (r g d) -> p r g d", r=4, g=NG), v[:, :, :, 0:HD],
                                        recip[:, q, :].rearrange("p (r g) -> p r g", g=NG).unsqueeze(3).broadcast_to([P, 4, NG, HD]),
                                        ALU.mult).then_inc(M0.free, 1)

            def add_residual():
                pr.read(M0)
                dve.wait_ge(loaded["x_res"], xres_n.step())
                nc.vector.tensor_tensor(x_res[:].rearrange("p q c -> p (q c)"), M0.ps[:],
                                        x_res[:].rearrange("p q c -> p (q c)"), ALU.add).then_inc(M0.free, 1)

            def split_gu(c):
                dve.wait_ge(gu_hi_done, c + 1)
                w = slice(512 * c, 512 * c + 512)
                nc.vector.tensor_tensor(gu_lo[:, w], gu_raw[:, w], gu_hi[:, w].bitcast(F32), ALU.subtract).then_inc(gu_split, 1)

            row_stats()
            mean_variance()
            add_eps()
            dve.wait_ge(S[0].free, pr.skip(S[0]))
            nc.vector.memset(dist[:, 0:127], MASKED).then_inc(dist_ready, 1)
            normalise()
            dve.wait_ge(attn_w_hi, 1)
            nc.vector.tensor_tensor(wqk_lo[:], wqk, wqk_hi[:].bitcast(F32), ALU.subtract).then_inc(attn_w_split, 1)
            pr.skip(M0)
            pr.skip(GATE)
            pr.skip(UP)
            dve.wait_ge(loaded["small"], 16 * 7)
            add_router_bias()
            largest_logit()
            compare_logits()
            shift_logits()
            equal_or_greater()
            greater()
            count_ahead()
            split_gu(0)
            split_gu(1)
            keep_top()
            sum_kept()
            invert_total()
            combine_weights()
            split_gu(2)
            split_gu(3)
            row_stats()
            mean_variance()
            add_eps()
            dve.wait_ge(filled, 4)
            pr.skip(M1)
            copy_v()
            for k in range(2):
                clip_up(k)
                activate(k)
            for c in range(4, 8):
                split_gu(c)
            normalise()
            for k in range(2, AHEAD - 1):
                clip_up(k)
                activate(k)
            dve.wait_ge(loaded["bias"], 16)

            def body(t, last):
                pr.begin(t)
                for k in range(AHEAD, CHUNKS):
                    heads = beside(k)
                    if k == AHEAD + 1:
                        dve.wait_ge(loaded["bias_rest"], 16 * (NG - 1))
                    for u in heads[:1]:
                        reduce_max(*u)
                    clip_up(k - 1)
                    for u in heads[1:2]:
                        reduce_max(*u)
                    activate(k - 1)
                    for u in heads[2:]:
                        reduce_max(*u)
                clip_up(CHUNKS - 1)
                activate(CHUNKS - 1)
                pr.skip(M1, 2)
                for u, b, r, g in units(0, 32):
                    if u == 0:
                        dve.wait_ge(loaded["bias_again"], 16 * NG)
                    add_bias(u, b, r, g)
                    if not last:
                        if u == 0:
                            pr.skip(M0)
                            pr.skip(GATE)
                            pr.skip(UP)
                        if u == 8:
                            add_router_bias()
                        if u == 9:
                            largest_logit()
                            compare_logits()
                        if u == 10:
                            shift_logits()
                            equal_or_greater()
                        if u == 11:
                            greater()
                        if u == 12:
                            count_ahead()
                        if u == 17:
                            keep_top()
                        if u == 18:
                            sum_kept()
                        if u == 19:
                            invert_total()
                        if u == 20:
                            combine_weights()
                        if u == 21:
                            row_stats()
                        if u == 22:
                            mean_variance()
                        if u == 23:
                            add_eps()
                    if u == 25:
                        norm_heads(0)
                    if u == 29:
                        norm_heads(1)
                pv_done = pv_n.step(P_SLOTS // 4)
                if not last:
                    pr.skip(M1)
                    dve.wait_ge(PV.full, pv_done)
                    copy_v()
                pr.skip(M1, 2)
                norm_heads(2)
                if not last:
                    clip_up(0)
                    activate(0)
                norm_heads(3)
                if not last:
                    for k in (1, 2):
                        clip_up(k)
                        activate(k)
                    normalise()
                    clip_up(3)
                    activate(3)
                add_residual()
                if not last:
                    clip_up(4)
                    activate(4)

            with dve.Fori(0, N - 1) as t:
                body(t, False)
            body(N - 1, True)

        @block.gpsimd
        def _(pool):
            pr = Program(pool)
            var_n, row_n = pr.count(var_ready, 1), pr.count(comb_row_loaded, 1, 16)
            act_n, free_n = pr.count(act_ready, CHUNKS), pr.count(slot_free, CHUNKS)
            all_n = pr.count(comb_all_ready, 1)

            def inverse_std():
                pool.wait_ge(var_ready, var_n.step())
                nc.gpsimd.tensor_tensor(rstd[:], var_eps[:], minus_half[:], ALU.pow).then_inc(rstd_ready, 1)

            def split_x():
                pool.wait_ge(M0.free, pr.skip(M0))
                nc.gpsimd.tensor_tensor(xn_lo[:], xn_t[:], xn_hi[:].bitcast(F32), ALU.subtract).then_inc(xn_split, 1)

            def reverse_x():
                nc.gpsimd.tensor_copy(xn_rev[:], xn_t[:, ::-1]).then_inc(xn_rev_ready, 1)

            def split_qk():
                for w, b in enumerate((GATE, UP)):
                    pool.wait_ge(b.free, pr.skip(b))
                    nc.gpsimd.tensor_tensor(qk_lo[:, w, :], qk[:, w, :], qk_hi[:, w, :].bitcast(F32),
                                            ALU.subtract).then_inc(qk_split, 1)

            def spread_combine():
                pr.wait(comb_row_loaded, row_n.step())
                for e in range(EXPERTS):
                    i = nc.gpsimd.partition_broadcast(comb_all[:, e, :], comb_all[0:1, e, :], P)
                i.then_inc(comb_all_ready, 1)
                pool.wait_ge(comb_all_ready, all_n.step())

            def weigh(k):
                pool.wait_ge(act_ready, act_n.step())
                pool.wait_ge(slot_free, free_n.step())
                nc.gpsimd.tensor_tensor(aw_buf[:, k % AW_SLOTS, :], s_buf[:, k % SU_SLOTS, :], comb_all[:, k // 2, :],
                                        ALU.mult).then_inc(weighted, 1)

            nc.gpsimd.memset(minus_half[:], -0.5).then_inc(pool_step, 1)
            pool.wait_ge(pool_step, 1)
            inverse_std()
            nc.gpsimd.memset(v_one[:], 0.0).then_inc(filled, 1)
            pool.wait_ge(filled, 1)
            nc.gpsimd.memset(v_heads[:, :, :, HD:HD + 1], 1.0).then_inc(filled, 1)
            split_x()
            nc.gpsimd.memset(q_rows[:].bitcast(F32), 0.0).then_inc(filled, 1)
            nc.gpsimd.memset(k_rows[:].bitcast(F32), 1.0).then_inc(filled, 1)
            split_qk()
            reverse_x()
            inverse_std()
            spread_combine()
            for k in range(AHEAD - 1):
                weigh(k)

            pr.skip(M0)
            pr.skip(GATE, AHEAD)
            pr.skip(UP, AHEAD)

            def body(t, last):
                pr.begin(t)
                for k in range(AHEAD - 1, CHUNKS):
                    weigh(k)
                pr.skip(GATE, CHUNKS - AHEAD)
                pr.skip(UP, CHUNKS - AHEAD)
                if not last:
                    split_x()
                    split_qk()
                    reverse_x()
                    inverse_std()
                    spread_combine()
                    pr.skip(M0, 6)
                    pr.skip(GATE, AHEAD)
                    pr.skip(UP, AHEAD)
                    for k in range(AHEAD - 1):
                        weigh(k)

            with pool.Fori(0, N - 1) as t:
                body(t, False)
            body(N - 1, True)


def distance_one_hots():
    n = np.arange(256)
    exact = BUCKETS // 2
    ratio = np.log(np.maximum(n, 1).astype(np.float32) / np.float32(exact)) / np.float32(math.log(MAX_DISTANCE / exact))
    large = np.minimum(exact + (ratio * np.float32(BUCKETS - exact)).astype(np.int32), BUCKETS - 1)
    bucket = np.where(n < exact, n, large)
    hot = np.zeros((BUCKETS, SPAN), np.float32)
    hot[bucket, 127 + n] = 1.0
    return hot


def kernel(**inputs):
    import concourse.bacc as bacc
    from concourse.bass_utils import run_bass_kernel_spmd

    a = {k.replace("L0_attn_", "").replace("L0_ffn_", ""): np.asarray(v) for k, v in inputs.items()}
    batch, seq, d = a["x"].shape

    def by_rows(w):
        return w.reshape(4, NG, HD, -1).transpose(0, 2, 1, 3).reshape(P, -1)

    arrays = {
        "x": a["x"].reshape(batch * seq, d),
        "wqk": np.stack([by_rows(a["Wq"]).T, by_rows(a["Wk"]).T], axis=1),
        "wv": a["Wv"].T,
        "wo_t": a["Wo"].T,
        "cols": np.stack([by_rows(a["bq"])[:, 0], by_rows(a["bk"])[:, 0], a["bo"]], axis=1),
        "bv": a["bv"],
        "rel": a["rel_emb"],
        "onehot": distance_one_hots(),
        "ident": np.eye(P, dtype=np.float32),
        "tri": np.tile(np.tril(np.ones((EXPERTS, EXPERTS), np.float32), -1).reshape(-1), TILES),
        "wr_t": a["router_weight"].T,
        "rb": a["router_bias"],
        "gu_t": a["gate_up_proj"].reshape(-1, d).T,
        "gu_bias": a["gate_up_proj_bias"].reshape(-1, P).T,
        "dn_t": a["down_proj"].reshape(EXPERTS, d, 2, P).transpose(3, 0, 2, 1).reshape(P, CHUNKS, d),
        "dn_bias": a["down_proj_bias"],
    }
    arrays = {k: np.ascontiguousarray(v) for k, v in arrays.items()}

    nc = bacc.Bacc("TRN2", target_bir_lowering=False, num_devices=1)
    ins = {k: nc.dram_tensor(f"in_{k}", v.shape, mybir.dt.from_np(v.dtype), kind="ExternalInput").ap()
           for k, v in arrays.items()}
    out = nc.dram_tensor("out_y", (batch * seq, d), F32, kind="ExternalOutput").ap()
    build_layer(nc, ins, out)
    r = run_bass_kernel_spmd(nc, [{f"in_{k}": v for k, v in arrays.items()}], core_ids=[0])
    return r.results[0]["out_y"].reshape(batch, seq, d)
```
